# Optimizing a Trainium2 kernel written in Bass

```python
import numpy as np
import jax
import jax.numpy as jnp

def _softmax(x, axis=-1):
    return jax.nn.softmax(x, axis=axis)

def _gelu(x):
    return jax.nn.gelu(x, approximate=True)

def _silu(x):
    return jax.nn.silu(x)

def _sigmoid(x):
    return jax.nn.sigmoid(x)

def _layernorm(x, axis=-1, eps=1e-05):
    m = jnp.mean(x, axis=axis, keepdims=True)
    v = jnp.var(x, axis=axis, keepdims=True)
    return (x - m) / jnp.sqrt(v + eps)

def _scatter_add(tgt, idx, src, axis=0):
    return tgt.at[idx].add(src)

def _segment_sum(src, seg, n):
    return jax.ops.segment_sum(src, seg, n)
kernel_name = 'mk_adaln_ffn_d2_seqx_r4_ce0903'

def setup_inputs(seed: int=0):
    np.random.seed(seed)
    _w = jnp.asarray

    def _rec_inputs():
        import jax
        import jax.numpy as jnp
        _rk = jax.random.key(seed)
        x = -0.000125 + 0.9999 * jax.random.normal(jax.random.fold_in(_rk, 1), (4, 512, 512), jnp.float32)
        _lenS = 512 - jax.random.randint(jax.random.fold_in(_rk, 7), (4,), 0, max(1, 512 // 4) + 1, jnp.int32)
        _lenS2 = 512 - jax.random.randint(jax.random.fold_in(_rk, 8), (4,), 0, max(1, 512 // 4) + 1, jnp.int32)
        fside_BxSxS_0 = -1.52775e-05 + 0.999936 * jax.random.normal(jax.random.fold_in(_rk, 11), (4, 512, 512), jnp.float32)
        cond_512 = -5.03954e-05 + 1.00559 * jax.random.normal(jax.random.fold_in(_rk, 12), (4, 128), jnp.float32)
        return (x, fside_BxSxS_0, cond_512)
    x, fside_BxSxS_0, cond_512 = _rec_inputs()

    def _L0_cond_setup():
        import jax, jax.numpy as jnp
        from jax import lax
        import numpy as np
        B, T, C, TD = (8, 512, 512, 128)

        def _bi_wkv(r, k, v, w, u, time_emb):
            tf = jax.nn.sigmoid(jnp.sum(time_emb, axis=-1))[:, None, None]
            decay = jnp.exp(-jnp.exp(w.astype(jnp.float32)))[None, :] * (0.5 + 0.5 * tf[:, :, 0])
            kf = k.astype(jnp.float32)
            vf = v.astype(jnp.float32)
            ek = jnp.exp(jnp.minimum(kf, 30.0))
            ekv = ek * vf

            def step(carry, x):
                a, b = carry
                ekv_t, ek_t = x
                a = a * decay + ekv_t
                b = b * decay + ek_t
                return ((a, b), (a, b))
            ekv_t = jnp.swapaxes(ekv, 0, 1)
            ek_t = jnp.swapaxes(ek, 0, 1)
            init = (jnp.zeros_like(decay), jnp.zeros_like(decay))
            _, (nf, df) = lax.scan(step, init, (ekv_t, ek_t))
            _, (nb, db) = lax.scan(step, init, (ekv_t, ek_t), reverse=True)
            nf = jnp.swapaxes(nf, 0, 1)
            df = jnp.swapaxes(df, 0, 1)
            nb = jnp.swapaxes(nb, 0, 1)
            db = jnp.swapaxes(db, 0, 1)
            euk = jnp.exp(jnp.minimum(u.astype(jnp.float32)[None, None, :] + kf, 30.0))
            num = nf + nb - ekv + euk * vf
            den = df + db - ek + euk
            base = jax.nn.sigmoid(r.astype(jnp.float32)) * (num / jnp.maximum(den, 1e-08))
            out = base * (0.8 + 0.2 * tf)
            return out.astype(r.dtype)
        key = jax.random.key(seed)
        ks = jax.random.split(key, 6)
        return {'r': jax.random.normal(ks[0], (B, T, C), dtype=jnp.float32), 'k': jax.random.normal(ks[1], (B, T, C), dtype=jnp.float32), 'v': jax.random.normal(ks[2], (B, T, C), dtype=jnp.float32), 'w': jax.random.normal(ks[3], (C,), dtype=jnp.float32), 'u': jax.random.normal(ks[4], (C,), dtype=jnp.float32), 'time_emb': jax.random.normal(ks[5], (B, TD), dtype=jnp.float32)}
    _L0_cond_all = _L0_cond_setup()
    _L0_cond_in = {k: v for k, v in _L0_cond_all.items() if k in ('w', 'u')}
    del _L0_cond_all

    def _L0_ffn_setup():
        import jax, jax.numpy as jnp
        import numpy as np
        B, S, D = (4, 512, 512)
        E, F, K = (8, 256, 2)
        SF = 256
        EPS = 1e-06

        def _rmsnorm(x, w, eps=EPS):
            var = jnp.mean(x * x, axis=-1, keepdims=True)
            return x * jax.lax.rsqrt(var + eps) * w
        key = jax.random.key(seed)
        ks = jax.random.split(key, 9)
        g = lambda k, shape, scale: jax.random.normal(k, shape, jnp.float32) * scale
        return {'x': g(ks[0], (B, S, D), 1.0), 'rms_weight': jnp.ones((D,), jnp.float32), 'router_w': g(ks[1], (D, E), 0.02), 'w_gate': g(ks[2], (E, D, F), 0.02), 'w_up': g(ks[3], (E, D, F), 0.02), 'w_down': g(ks[4], (E, F, D), 0.02), 'sw_gate': g(ks[5], (D, SF), 0.02), 'sw_up': g(ks[6], (D, SF), 0.02), 'sw_down': g(ks[7], (SF, D), 0.02)}
    _L0_ffn_all = _L0_ffn_setup()
    _L0_ffn_in = {k: v for k, v in _L0_ffn_all.items() if k in ('rms_weight', 'router_w', 'w_gate', 'w_up', 'w_down', 'sw_gate', 'sw_up', 'sw_down')}
    del _L0_ffn_all

    def _L1_cond_setup():
        import jax, jax.numpy as jnp
        from jax import lax
        import numpy as np
        B, T, C, TD = (8, 512, 512, 128)

        def _bi_wkv(r, k, v, w, u, time_emb):
            tf = jax.nn.sigmoid(jnp.sum(time_emb, axis=-1))[:, None, None]
            decay = jnp.exp(-jnp.exp(w.astype(jnp.float32)))[None, :] * (0.5 + 0.5 * tf[:, :, 0])
            kf = k.astype(jnp.float32)
            vf = v.astype(jnp.float32)
            ek = jnp.exp(jnp.minimum(kf, 30.0))
            ekv = ek * vf

            def step(carry, x):
                a, b = carry
                ekv_t, ek_t = x
                a = a * decay + ekv_t
                b = b * decay + ek_t
                return ((a, b), (a, b))
            ekv_t = jnp.swapaxes(ekv, 0, 1)
            ek_t = jnp.swapaxes(ek, 0, 1)
            init = (jnp.zeros_like(decay), jnp.zeros_like(decay))
            _, (nf, df) = lax.scan(step, init, (ekv_t, ek_t))
            _, (nb, db) = lax.scan(step, init, (ekv_t, ek_t), reverse=True)
            nf = jnp.swapaxes(nf, 0, 1)
            df = jnp.swapaxes(df, 0, 1)
            nb = jnp.swapaxes(nb, 0, 1)
            db = jnp.swapaxes(db, 0, 1)
            euk = jnp.exp(jnp.minimum(u.astype(jnp.float32)[None, None, :] + kf, 30.0))
            num = nf + nb - ekv + euk * vf
            den = df + db - ek + euk
            base = jax.nn.sigmoid(r.astype(jnp.float32)) * (num / jnp.maximum(den, 1e-08))
            out = base * (0.8 + 0.2 * tf)
            return out.astype(r.dtype)
        key = jax.random.key(seed)
        ks = jax.random.split(key, 6)
        return {'r': jax.random.normal(ks[0], (B, T, C), dtype=jnp.float32), 'k': jax.random.normal(ks[1], (B, T, C), dtype=jnp.float32), 'v': jax.random.normal(ks[2], (B, T, C), dtype=jnp.float32), 'w': jax.random.normal(ks[3], (C,), dtype=jnp.float32), 'u': jax.random.normal(ks[4], (C,), dtype=jnp.float32), 'time_emb': jax.random.normal(ks[5], (B, TD), dtype=jnp.float32)}
    _L1_cond_all = _L1_cond_setup()
    _L1_cond_in = {k: v for k, v in _L1_cond_all.items() if k in ('w', 'u')}
    del _L1_cond_all

    def _L1_ffn_setup():
        import jax, jax.numpy as jnp
        import numpy as np
        from jax import lax
        DIM = 512
        INTER = 352
        N_EXPERTS = 32
        TOP_K = 6
        N_SHARED = 2
        CAPACITY = 512
        ROUTE_SCALE = 1.0

        def _gate(xf, gate_w):
            logits = xf @ gate_w.T
            scores = jax.nn.softmax(logits.astype(jnp.float32), axis=-1)
            top_w, top_i = lax.top_k(scores, TOP_K)
            return ((top_w * ROUTE_SCALE).astype(xf.dtype), top_i)

        def _moe(xf, gate_w, w1, w2, w3):
            T, D = xf.shape
            E, CAP = (N_EXPERTS, CAPACITY)
            top_w, top_i = _gate(xf, gate_w)
            e_flat = top_i.reshape(-1)
            t_flat = jnp.repeat(jnp.arange(T), TOP_K)
            w_flat = top_w.reshape(-1)
            order = jnp.argsort(e_flat)
            e_s, t_s, w_s = (e_flat[order], t_flat[order], w_flat[order])
            counts = jnp.zeros((E,), jnp.int32).at[e_s].add(1)
            starts = jnp.concatenate([jnp.zeros((1,), jnp.int32), jnp.cumsum(counts)[:-1]])
            pos = jnp.arange(T * TOP_K, dtype=jnp.int32) - starts[e_s]
            valid = pos < CAP
            buf_idx = jnp.where(valid, e_s * CAP + pos, E * CAP)
            xbuf = jnp.zeros((E * CAP + 1, D), xf.dtype).at[buf_idx].set(xf[t_s])
            xb = xbuf[:E * CAP].reshape(E, CAP, D)
            h = jax.nn.silu(jnp.einsum('ecd,edi->eci', xb, w1)) * jnp.einsum('ecd,edi->eci', xb, w3)
            ob = jnp.einsum('eci,eid->ecd', h, w2).reshape(E * CAP, D)
            ob = jnp.concatenate([ob, jnp.zeros((1, D), ob.dtype)], axis=0)
            y_pairs = ob[buf_idx] * w_s[:, None]
            y = jnp.zeros((T, D), xf.dtype).at[t_s].add(y_pairs)
            return y
        key = jax.random.key(seed)
        ks = jax.random.split(key, 9)
        B, S = (4, 512)
        si = INTER * N_SHARED
        inputs = {'x': jax.random.normal(ks[0], (B, S, DIM), jnp.float32), 'gate_w': jax.random.normal(ks[1], (N_EXPERTS, DIM), jnp.float32), 'w1': jax.random.normal(ks[2], (N_EXPERTS, DIM, INTER), jnp.float32) * DIM ** (-0.5), 'w2': jax.random.normal(ks[3], (N_EXPERTS, INTER, DIM), jnp.float32) * INTER ** (-0.5), 'w3': jax.random.normal(ks[4], (N_EXPERTS, DIM, INTER), jnp.float32) * DIM ** (-0.5), 'sw1': jax.random.normal(ks[5], (DIM, si), jnp.float32) * DIM ** (-0.5), 'sw2': jax.random.normal(ks[6], (si, DIM), jnp.float32) * si ** (-0.5), 'sw3': jax.random.normal(ks[7], (DIM, si), jnp.float32) * DIM ** (-0.5)}
        return inputs
    _L1_ffn_all = _L1_ffn_setup()
    _L1_ffn_in = {k: v for k, v in _L1_ffn_all.items() if k in ('gate_w', 'w1', 'w2', 'w3', 'sw1', 'sw2', 'sw3')}
    del _L1_ffn_all
    return {'x': x, 'fside_BxSxS_0': fside_BxSxS_0, 'cond_512': cond_512, 'L0_cond_w': _L0_cond_in['w'], 'L0_cond_u': _L0_cond_in['u'], 'L0_ffn_rms_weight': _L0_ffn_in['rms_weight'], 'L0_ffn_router_w': _L0_ffn_in['router_w'], 'L0_ffn_w_gate': _L0_ffn_in['w_gate'], 'L0_ffn_w_up': _L0_ffn_in['w_up'], 'L0_ffn_w_down': _L0_ffn_in['w_down'], 'L0_ffn_sw_gate': _L0_ffn_in['sw_gate'], 'L0_ffn_sw_up': _L0_ffn_in['sw_up'], 'L0_ffn_sw_down': _L0_ffn_in['sw_down'], 'L1_cond_w': _L1_cond_in['w'], 'L1_cond_u': _L1_cond_in['u'], 'L1_ffn_gate_w': _L1_ffn_in['gate_w'], 'L1_ffn_w1': _L1_ffn_in['w1'], 'L1_ffn_w2': _L1_ffn_in['w2'], 'L1_ffn_w3': _L1_ffn_in['w3'], 'L1_ffn_sw1': _L1_ffn_in['sw1'], 'L1_ffn_sw2': _L1_ffn_in['sw2'], 'L1_ffn_sw3': _L1_ffn_in['sw3']}

def reference(x, fside_BxSxS_0, cond_512, L0_cond_w, L0_cond_u, L0_ffn_rms_weight, L0_ffn_router_w, L0_ffn_w_gate, L0_ffn_w_up, L0_ffn_w_down, L0_ffn_sw_gate, L0_ffn_sw_up, L0_ffn_sw_down, L1_cond_w, L1_cond_u, L1_ffn_gate_w, L1_ffn_w1, L1_ffn_w2, L1_ffn_w3, L1_ffn_sw1, L1_ffn_sw2, L1_ffn_sw3):
    import jax
    import jax.numpy as jnp

    def _L0_cond_ref(r, k, v, w, u, time_emb):
        import jax, jax.numpy as jnp
        from jax import lax
        import numpy as np
        B, T, C, TD = (8, 512, 512, 128)

        def _bi_wkv(r, k, v, w, u, time_emb):
            tf = jax.nn.sigmoid(jnp.sum(time_emb, axis=-1))[:, None, None]
            decay = jnp.exp(-jnp.exp(w.astype(jnp.float32)))[None, :] * (0.5 + 0.5 * tf[:, :, 0])
            kf = k.astype(jnp.float32)
            vf = v.astype(jnp.float32)
            ek = jnp.exp(jnp.minimum(kf, 30.0))
            ekv = ek * vf

            def step(carry, x):
                a, b = carry
                ekv_t, ek_t = x
                a = a * decay + ekv_t
                b = b * decay + ek_t
                return ((a, b), (a, b))
            ekv_t = jnp.swapaxes(ekv, 0, 1)
            ek_t = jnp.swapaxes(ek, 0, 1)
            init = (jnp.zeros_like(decay), jnp.zeros_like(decay))
            _, (nf, df) = lax.scan(step, init, (ekv_t, ek_t))
            _, (nb, db) = lax.scan(step, init, (ekv_t, ek_t), reverse=True)
            nf = jnp.swapaxes(nf, 0, 1)
            df = jnp.swapaxes(df, 0, 1)
            nb = jnp.swapaxes(nb, 0, 1)
            db = jnp.swapaxes(db, 0, 1)
            euk = jnp.exp(jnp.minimum(u.astype(jnp.float32)[None, None, :] + kf, 30.0))
            num = nf + nb - ekv + euk * vf
            den = df + db - ek + euk
            base = jax.nn.sigmoid(r.astype(jnp.float32)) * (num / jnp.maximum(den, 1e-08))
            out = base * (0.8 + 0.2 * tf)
            return out.astype(r.dtype)
        return _bi_wkv(r, k, v, w, u, time_emb)

    def _L0_ffn_ref(x, rms_weight, router_w, w_gate, w_up, w_down, sw_gate, sw_up, sw_down):
        import jax, jax.numpy as jnp
        import numpy as np
        B, S, D = (4, 512, 512)
        E, F, K = (8, 256, 2)
        SF = 256
        EPS = 1e-06

        def _rmsnorm(x, w, eps=EPS):
            var = jnp.mean(x * x, axis=-1, keepdims=True)
            return x * jax.lax.rsqrt(var + eps) * w
        b, s, d = x.shape
        e = router_w.shape[1]
        h = _rmsnorm(x, rms_weight)
        ht = h.reshape(-1, d)
        t = ht.shape[0]
        logits = ht @ router_w
        probs = jax.nn.softmax(logits, axis=-1)
        topv, topi = jax.lax.top_k(probs, K)
        topv = topv / jnp.sum(topv, axis=-1, keepdims=True)
        w_dense = jnp.zeros((t, e), ht.dtype).at[jnp.arange(t)[:, None], topi].set(topv)
        g = jnp.einsum('td,edf->tef', ht, w_gate)
        u = jnp.einsum('td,edf->tef', ht, w_up)
        eo = jnp.einsum('tef,efd->ted', jax.nn.silu(g) * u, w_down)
        moe = jnp.einsum('te,ted->td', w_dense, eo)
        sh = jax.nn.silu(ht @ sw_gate) * (ht @ sw_up) @ sw_down
        return (moe + sh).reshape(b, s, d)

    def _L1_cond_ref(r, k, v, w, u, time_emb):
        import jax, jax.numpy as jnp
        from jax import lax
        import numpy as np
        B, T, C, TD = (8, 512, 512, 128)

        def _bi_wkv(r, k, v, w, u, time_emb):
            tf = jax.nn.sigmoid(jnp.sum(time_emb, axis=-1))[:, None, None]
            decay = jnp.exp(-jnp.exp(w.astype(jnp.float32)))[None, :] * (0.5 + 0.5 * tf[:, :, 0])
            kf = k.astype(jnp.float32)
            vf = v.astype(jnp.float32)
            ek = jnp.exp(jnp.minimum(kf, 30.0))
            ekv = ek * vf

            def step(carry, x):
                a, b = carry
                ekv_t, ek_t = x
                a = a * decay + ekv_t
                b = b * decay + ek_t
                return ((a, b), (a, b))
            ekv_t = jnp.swapaxes(ekv, 0, 1)
            ek_t = jnp.swapaxes(ek, 0, 1)
            init = (jnp.zeros_like(decay), jnp.zeros_like(decay))
            _, (nf, df) = lax.scan(step, init, (ekv_t, ek_t))
            _, (nb, db) = lax.scan(step, init, (ekv_t, ek_t), reverse=True)
            nf = jnp.swapaxes(nf, 0, 1)
            df = jnp.swapaxes(df, 0, 1)
            nb = jnp.swapaxes(nb, 0, 1)
            db = jnp.swapaxes(db, 0, 1)
            euk = jnp.exp(jnp.minimum(u.astype(jnp.float32)[None, None, :] + kf, 30.0))
            num = nf + nb - ekv + euk * vf
            den = df + db - ek + euk
            base = jax.nn.sigmoid(r.astype(jnp.float32)) * (num / jnp.maximum(den, 1e-08))
            out = base * (0.8 + 0.2 * tf)
            return out.astype(r.dtype)
        return _bi_wkv(r, k, v, w, u, time_emb)

    def _L1_ffn_ref(x, gate_w, w1, w2, w3, sw1, sw2, sw3):
        import jax, jax.numpy as jnp
        import numpy as np
        from jax import lax
        DIM = 512
        INTER = 352
        N_EXPERTS = 32
        TOP_K = 6
        N_SHARED = 2
        CAPACITY = 512
        ROUTE_SCALE = 1.0

        def _gate(xf, gate_w):
            logits = xf @ gate_w.T
            scores = jax.nn.softmax(logits.astype(jnp.float32), axis=-1)
            top_w, top_i = lax.top_k(scores, TOP_K)
            return ((top_w * ROUTE_SCALE).astype(xf.dtype), top_i)

        def _moe(xf, gate_w, w1, w2, w3):
            T, D = xf.shape
            E, CAP = (N_EXPERTS, CAPACITY)
            top_w, top_i = _gate(xf, gate_w)
            e_flat = top_i.reshape(-1)
            t_flat = jnp.repeat(jnp.arange(T), TOP_K)
            w_flat = top_w.reshape(-1)
            order = jnp.argsort(e_flat)
            e_s, t_s, w_s = (e_flat[order], t_flat[order], w_flat[order])
            counts = jnp.zeros((E,), jnp.int32).at[e_s].add(1)
            starts = jnp.concatenate([jnp.zeros((1,), jnp.int32), jnp.cumsum(counts)[:-1]])
            pos = jnp.arange(T * TOP_K, dtype=jnp.int32) - starts[e_s]
            valid = pos < CAP
            buf_idx = jnp.where(valid, e_s * CAP + pos, E * CAP)
            xbuf = jnp.zeros((E * CAP + 1, D), xf.dtype).at[buf_idx].set(xf[t_s])
            xb = xbuf[:E * CAP].reshape(E, CAP, D)
            h = jax.nn.silu(jnp.einsum('ecd,edi->eci', xb, w1)) * jnp.einsum('ecd,edi->eci', xb, w3)
            ob = jnp.einsum('eci,eid->ecd', h, w2).reshape(E * CAP, D)
            ob = jnp.concatenate([ob, jnp.zeros((1, D), ob.dtype)], axis=0)
            y_pairs = ob[buf_idx] * w_s[:, None]
            y = jnp.zeros((T, D), xf.dtype).at[t_s].add(y_pairs)
            return y
        shape = x.shape
        xf = x.reshape(-1, DIM)
        y = _moe(xf, gate_w, w1, w2, w3)
        shared = jax.nn.silu(xf @ sw1) * (xf @ sw3) @ sw2
        return (y + shared).reshape(shape)
    x = x + _L0_ffn_ref(_L0_cond_ref(x, fside_BxSxS_0, fside_BxSxS_0, L0_cond_w, L0_cond_u, cond_512), L0_ffn_rms_weight, L0_ffn_router_w, L0_ffn_w_gate, L0_ffn_w_up, L0_ffn_w_down, L0_ffn_sw_gate, L0_ffn_sw_up, L0_ffn_sw_down)
    x = x + _L1_ffn_ref(_L1_cond_ref(x, fside_BxSxS_0, fside_BxSxS_0, L1_cond_w, L1_cond_u, cond_512), L1_ffn_gate_w, L1_ffn_w1, L1_ffn_w2, L1_ffn_w3, L1_ffn_sw1, L1_ffn_sw2, L1_ffn_sw3)
    return x

_drawn_inputs = setup_inputs


def setup_inputs(seed=0):
    import zlib

    import numpy as np

    out = dict(_drawn_inputs(seed))
    spreads = {'L0_ffn_rms_weight': (1.0, 0.6)}
    factors = {'L0_cond_u': 4.756}
    for name, (base, spread) in spreads.items():
        noise = np.random.default_rng([zlib.crc32(name.encode()), seed]).standard_normal(out[name].shape)
        drawn = base * np.exp(spread * noise) if base else spread * noise
        out[name] = jnp.asarray(drawn.astype(out[name].dtype))
    for name, factor in factors.items():
        out[name] = (out[name] * factor).astype(out[name].dtype)
    return out
```

```python
from contextlib import ExitStack

import concourse.bass as bass
from concourse import mybir

P = 128
T = 2048
D = 512
NT = T // P
ROWS = T + 512
CAP = 512
F32 = mybir.dt.float32
F16 = mybir.dt.float16
I32 = mybir.dt.int32
U32 = mybir.dt.uint32
ALU = mybir.AluOpType
ACT = mybir.ActivationFunctionType
AX_X = mybir.AxisListType.X

XS = 8.0
WS = 64.0
UN = 1.0 / (XS * WS)

LAYERS = (
    dict(E=8, K=2, F=256, NK=2, NB=39, W=3072),
    dict(E=32, K=6, F=352, NK=3, NB=128, W=4352),
)
WCH = (((0, 1024), (1024, 1024), (2048, 1024)), ((0, 1088), (1088, 1088), (2176, 1088), (3264, 1088)))


class Line:

    def __init__(self, sem):
        self.sem, self.n, self.todo, self.seen = sem, 0, [], {}

    def wait(self, after):
        for tok in after:
            if tok is None:
                continue
            sem, v = tok
            if self.seen.get(id(sem), 0) < v:
                self.seen[id(sem)] = v
                self.todo.append((0, sem, v))

    def put(self, fn, *after):
        self.wait(after)
        self.n += 1
        self.todo.append((1, fn, (self.sem, 1)))
        return self.sem, self.n

    def then(self, fn, *after):
        return self.put(fn, (self.sem, self.n) if self.n else None, *after)

    def run(self, eng):
        for kind, a, b in self.todo:
            if kind == 0:
                eng.wait_ge(a, b)
            elif kind == 2:
                a()
            else:
                a().then_inc(*b)


class Ring:

    def __init__(self, sems):
        self.sems, self.v = sems, [0] * len(sems)

    def start(self, line, slot, fn, *after):
        line.wait(after)
        self.v[slot] += 16
        line.todo.append((1, fn, (self.sems[slot], 16)))
        return self.sems[slot], self.v[slot]


def build(nc, xtok, fT, cst, svec, cond, rms, rout, gatew, W0, W1, Y1):
    with ExitStack() as ctx:
        ctx.enter_context(nc.allow_low_precision(reason="sums of at most 16 ones are exact in float16"))

        def sb(name, shape, dt=F32):
            return ctx.enter_context(nc.sbuf_tensor(name, shape, dt))

        def sem(name):
            return ctx.enter_context(nc.semaphore(name))

        def ring(name, n):
            return Ring([sem(f"{name}{i}") for i in range(n)])

        X = [nc.dram_tensor(f"xrows{l}", [ROWS, D + LAYERS[l]["E"]], F32, kind="Internal").ap() for l in range(2)]
        Y0 = nc.dram_tensor("y0rows", [ROWS, D], F32, kind="Internal").ap()
        RT1 = nc.dram_tensor("ratio1", [T, D], F32, kind="Internal").ap()
        Y = [Y0, Y1]

        psG = [[ctx.enter_context(nc.psum_tensor(f"psG{a}{c}", [P, 512], F32)) for c in range(2)] for a in range(2)]
        psX = ctx.enter_context(nc.psum_tensor("psX", [P, 512], F32))
        psH = ctx.enter_context(nc.psum_tensor("psH", [P, 512], F32))
        psO = [ctx.enter_context(nc.psum_tensor(f"psO{a}", [P, 512], F32)) for a in range(2)]

        C = sb("C", [P, 528])
        ident, iota, U32f, dconst, tid = C[:, 0:128], C[:, 128:256], C[:, 256:384], C[:, 384:512], C[:, 512:528]
        iota16 = sb("iota16", [P, 128], F16)
        U16 = sb("U16", [P, 128], F16)
        ones16 = sb("ones16", [P, 128], F16)
        ones = sb("ones", [P, 8])
        half = sb("half", [P, 1])
        sv = sb("sv", [P, 16])
        rmsb = sb("rmsb", [P, D])
        rw = [sb("rw0", [P, 4, 8]), sb("rw1", [P, 4, 32])]
        dec = sb("dec", [P, 2, 4, 4])
        cs = sb("cs", [P, 8, 8])

        Whi = sb("Whi", [P, 8 * 3072], F16)
        Wlo = sb("Wlo", [P, 8 * 3072], F16)
        ST = [sb(f"ST{i}", [P, 1088]) for i in range(2)]

        WK = [{n: sb(f"wk{n}{i}", [P, 512]) for n in ("K", "EK", "EU", "EKV", "NF", "DF")} for i in range(2)]
        RT = [sb(f"RT{i}", [P, 4, 512]) for i in range(2)]
        XT = [sb(f"XT{i}", [P, 512]) for i in range(4)]
        BS = sb("BS", [P, 512])
        XR = [sb(f"XR{i}", [P, 512]) for i in range(2)]
        HT32 = sb("HT32", [P, 512])
        cnd = HT32[:, :].rearrange("p (b k) -> p b k", b=4)
        sm = sb("sm", [P, NT, 4])
        XSp = [sb(f"XSp{i}", [P, 2, 512], F16) for i in range(4)]
        XG = [sb(f"XG{i}", [P, D + 32]) for i in range(3)]
        zero = XG[0]
        WSL = sb("WSL", [P, 8])
        jnk = sb("jnk", [P, 8])
        H32 = [sb(f"H32{i}", [P, 384]) for i in range(2)]
        HS = [sb(f"HS{i}", [P, 2, 384], F16) for i in range(2)]
        OB = [sb(f"OB{i}", [P, 512]) for i in range(4)]

        lg = sb("lg", [P, 4, 32])
        mx = sb("mx", [P, 4, 8])
        ix = sb("ix", [P, 4, 8], U32)
        ixf = sb("ixf", [P, 4, 8])
        ex = sb("ex", [P, 4, 32])
        et = sb("et", [P, 4, 8])
        s1 = sb("s1", [P, 4, 1])
        s2 = sb("s2", [P, 4, 1])
        OH = sb("OH", [P, 4 * 6 * 32])
        OT = sb("OT", [P, 4 * 6 * 32])
        mask = sb("mask", [P, 4, 32], F16)
        mred = sb("mred", [P, 32], F16)
        macc = [sb(f"macc{i}", [P, 32], F16) for i in range(5)]
        Wd = [sb(f"Wd{i}", [P, 4, 32]) for i in range(2)]
        posb = sb("posb", [P, 16 * 8])
        gq = sb("gq", [P, 96])
        gi = sb("gi", [P, 96], I32)
        gj = sb("gj", [P, 96])
        qa = sb("qa", [P, 96])
        ja = sb("ja", [P, 96])
        cn = sb("cn", [P, 4, 8])
        cni = sb("cni", [P, 8], I32)
        ebf = sb("ebf", [P, 39])
        ebi = gi[:, 48:87]
        ohB = sb("ohB", [P, 39, 8], F16)
        AB = [RT[1][:, i, :].bitcast(F16).rearrange("p (a r n) -> p a r n", a=2, r=4) for i in range(2)]
        A16, B16 = [v[:, 0] for v in AB], [v[:, 1] for v in AB]
        idf = U32f
        idx = [sb("idx0", [P, 39], U32), posb[:, :].bitcast(U32)]

        pe, act, dve, pool, sp = (Line(sem(n)) for n in ("s_pe", "s_act", "s_dve", "s_pool", "s_sp"))
        s_c, s_z = ring("s_c", 1), ring("s_z", 1)
        r_k, r_x, r_st, r_g, r_o = ring("r_k", 2), ring("r_x", 4), ring("r_st", 2), ring("r_g", 3), ring("r_o", 4)
        r_rt1, r_rtl, r_y = ring("r_rt1", 1), ring("r_rtl", 2), ring("r_y", 4)
        r_xr = [ring("r_xr0", 2), ring("r_xr1", 2)]
        r_wd = [ring("r_wd0", 2), ring("r_wd1", 2)]
        V, A, G = nc.vector, nc.scalar, nc.gpsimd
        S = nc.sync

        for dst, src in ((C[:, :], cst), (sv[:, :], svec), (cnd[:, :, :], cond), (rmsb[:, :], rms),
                         (rw[0][:, :, :], rout), (rw[1][:, :, :], gatew)):
            t_c = s_c.start(sp, 0, lambda d=dst, s=src: S.dma_start(d, s))
        t_z = dve.put(lambda: V.memset(zero[:, :], 0.0))
        dve.put(lambda: V.memset(ones16[:, :], 1.0))
        dve.put(lambda: V.memset(ones[:, :], 1.0))
        t_half = dve.put(lambda: V.memset(half[:, :], -0.5))
        for h in H32:
            dve.put(lambda h=h: V.memset(h[:, :], 0.0))
        dve.put(lambda: V.tensor_copy(iota16[:, :], iota), t_c)
        t_c16 = dve.put(lambda: V.tensor_copy(U16[:, :], U32f))
        for k in range(4):
            rows = slice(T + P * k, T + P * k + P)
            for dst, w in ((X[0], D + 8), (X[1], D + 32), (Y[0], D), (Y[1], D)):
                t_dummy = s_z.start(sp, 0, lambda d=dst, r=rows, w=w: S.dma_start(d[r, :], zero[:, 0:w]), t_z)

        t = dve.then(lambda: V.tensor_reduce(cs[:, 0, 0:4], cnd[:, :, :], AX_X, ALU.add), t_c)
        t = act.put(lambda: A.activation(cs[:, 1, 0:4], cs[:, 0, 0:4], ACT.Exp, scale=-1.0), t)
        t = dve.then(lambda: V.tensor_scalar(cs[:, 2, 0:4], cs[:, 1, 0:4], 1.0, None, ALU.add), t)
        t = dve.then(lambda: V.reciprocal(cs[:, 3, 0:4], cs[:, 2, 0:4]), t)
        dve.then(lambda: V.tensor_scalar(cs[:, 4, 0:4], cs[:, 3, 0:4], 0.5, 0.5, ALU.mult, ALU.add), t)
        t_cs = dve.then(lambda: V.tensor_scalar(cs[:, 5, 0:4], cs[:, 3, 0:4], 0.2, 0.8, ALU.mult, ALU.add))
        t = act.put(lambda: A.activation(cs[:, 6, :], sv[:, 0:8], ACT.Exp), t_c)
        t_w = act.put(lambda: A.activation(cs[:, 7, :], cs[:, 6, :], ACT.Exp, scale=-1.0), t)
        for l in range(2):
            for c in range(4):
                t_dec = dve.then(lambda l=l, c=c: V.tensor_scalar(dec[:, l, c, :], cs[:, 4, 0:4],
                                                                 cs[:, 7, 4 * l + c:4 * l + c + 1], None, ALU.mult),
                                t_w, t_cs)

        wk = dict(n=0, free=[None, None], kfree=[None, None], psfree=None, rt=0)
        RTready, RTfree = {}, [[None], [None]]

        def wkv(l, b, c, ps, psbusy):
            n = wk["n"]
            wk["n"] += 1
            s = n % 2
            B = WK[s]
            k = B["K"]
            t_k = r_k.start(sp, s, lambda: S.dma_start(k[:, :], fT[c * P:c * P + P, b * 512:b * 512 + 512]),
                            wk["kfree"][s])
            u = sv[:, 8 + 4 * l + c:9 + 4 * l + c]
            dc = dec[:, l, c, b:b + 1].to_broadcast([P, 512])
            a0 = dve.put(lambda: V.tensor_scalar(B["EK"][:, :], k[:, :], 30.0, None, ALU.min), t_k, wk["free"][s])
            a1 = dve.put(lambda: V.tensor_scalar(B["EU"][:, :], k[:, :], u, 30.0, ALU.add, ALU.min))
            e0 = act.put(lambda: A.activation(B["EK"][:, :], B["EK"][:, :], ACT.Exp), a0)
            e1 = act.put(lambda: A.activation(B["EU"][:, :], B["EU"][:, :], ACT.Exp), a1)
            p0 = pool.put(lambda: G.tensor_tensor(B["EKV"][:, :], B["EK"][:, :], k[:, :], ALU.mult), e0, wk["free"][s])
            p1 = pool.put(lambda: G.tensor_tensor(B["EU"][:, :], B["EU"][:, :], B["EK"][:, :], ALU.subtract), e1)
            p2 = pool.put(lambda: G.tensor_tensor(k[:, :], B["EU"][:, :], k[:, :], ALU.mult), p1, p0)
            dve.put(lambda: V.tensor_tensor_scan(B["DF"][:, :], dc, B["EK"][:, :], 0.0, ALU.mult, ALU.add), e0, t_dec)
            d1 = dve.then(lambda: V.tensor_tensor_scan(B["EK"][:, ::-1], dc, B["EK"][:, ::-1], 0.0, ALU.mult, ALU.add), p1)
            dve.put(lambda: V.tensor_tensor_scan(B["NF"][:, :], dc, B["EKV"][:, :], 0.0, ALU.mult, ALU.add), p0)
            d3 = dve.then(lambda: V.tensor_tensor_scan(B["EKV"][:, ::-1], dc, B["EKV"][:, ::-1], 0.0, ALU.mult, ALU.add))
            q0 = pool.put(lambda: G.tensor_tensor(B["NF"][:, :], B["NF"][:, :], B["EKV"][:, :], ALU.add), d3)
            q1 = pool.put(lambda: G.tensor_tensor(B["NF"][:, :], B["NF"][:, :], k[:, :], ALU.add), q0, p2)
            wk["kfree"][s] = q1
            t1 = dve.put(lambda: V.tensor_tensor(B["DF"][:, :], B["DF"][:, :], B["EK"][:, :], ALU.add), d1)
            t2 = dve.put(lambda: V.tensor_tensor(B["DF"][:, :], B["DF"][:, :], B["EU"][:, :], ALU.add), t1, p1)
            t3 = dve.put(lambda: V.tensor_scalar(B["DF"][:, :], B["DF"][:, :], 1e-8, None, ALU.max), t2)
            t4 = dve.put(lambda: V.reciprocal(B["DF"][:, :], B["DF"][:, :]), t3)
            t5 = dve.put(lambda: V.scalar_tensor_tensor(out=B["NF"][:, :], in0=B["NF"][:, :], scalar=cs[:, 5, b:b + 1],
                                                        in1=B["DF"][:, :], op0=ALU.mult, op1=ALU.mult), t4, q1, t_cs)

            def tr():
                for q in range(4):
                    m = nc.tensor.transpose(ps[:, q * P:q * P + P], B["NF"][:, q * P:q * P + P], ident)
                return m
            m = pe.put(tr, t5, t_c, psbusy, wk["psfree"])
            wk["free"][s] = m
            h = wk["rt"] % 2
            after = RTfree[h] if c == 0 else []
            e = act.put(lambda: A.copy(RT[h][:, :, c * P:c * P + P], ps[:, :].rearrange("p (q c) -> p q c", q=4)),
                        m, *after)
            wk["psfree"] = e
            if c == 3:
                wk["rt"] += 1
                RTready[l, b] = (h, e)
                if l == 1:
                    w = r_rt1.start(sp, 0, lambda: S.dma_start(
                        RT1[b * 512:b * 512 + 512, :].rearrange("(q p) c -> p q c", p=P), RT[h][:, :, :]), e)
                    RTfree[h] = [w]
                    return w

        xs = dict(n=0, free=[None] * len(XSp))
        xt = dict(n=0, free=[None] * len(XT))
        fr = dict(bs=None, xr=[None, None], ht=None, lg=None, ps=None, pl=None)
        tile_xs, tile_x, lgt = {}, {}, {}

        def load_x(l, i, *after):
            s = xt["n"] % len(XT)
            xt["n"] += 1
            src = (xtok if l == 0 else Y0)[i * P:i * P + P, :]
            tile_x[l, i] = (s, r_x.start(sp, s, lambda: S.dma_start(XT[s][:, :], src), xt["free"][s], *after))

        def front(l, i, rt, t_rt, ps, psl, *after):
            s, t_x = tile_x[l, i]
            o = i % 2
            a = act.put(lambda: A.activation(BS[:, :], XT[s][:, :], ACT.Exp, scale=-1.0), t_x, fr["bs"])
            a = dve.put(lambda: V.tensor_scalar(BS[:, :], BS[:, :], 1.0, None, ALU.add), a)
            a = dve.put(lambda: V.reciprocal(BS[:, :], BS[:, :]), a)
            if l == 0:
                a = dve.put(lambda: V.tensor_tensor(BS[:, :], BS[:, :], rt, ALU.mult), a, t_rt)
                b = act.put(lambda: A.activation(XR[o][:, :], BS[:, :], ACT.Square, accum_out=sm[:, i, 0:1]),
                            a, *(fr["xr"][o] or ()))
                b = dve.put(lambda: V.tensor_scalar(sm[:, i, 1:2], sm[:, i, 0:1], 1.0 / D, 1e-6, ALU.mult, ALU.add), b)
                b = pool.put(lambda: G.tensor_tensor(sm[:, i, 2:3], sm[:, i, 1:2], half[:, :], ALU.pow), b, t_half)
                a = dve.put(lambda: V.scalar_tensor_tensor(out=XR[o][:, :], in0=BS[:, :], scalar=sm[:, i, 2:3],
                                                           in1=rmsb[:, :], op0=ALU.mult, op1=ALU.mult), b, t_c)
            else:
                a = dve.put(lambda: V.tensor_tensor(XR[o][:, :], BS[:, :], rt, ALU.mult), a, t_rt,
                            *(fr["xr"][o] or ()))
            fr["bs"] = a
            w = r_xr[l].start(sp, o, lambda: S.dma_start(X[l][i * P:i * P + P, 0:D], XR[o][:, :]), a)

            def tr():
                for q in range(4):
                    m = nc.tensor.transpose(ps[:, q * P:q * P + P], XR[o][:, q * P:q * P + P], ident)
                return m
            m = pe.put(tr, a, fr["ps"], fr["pl"], *after)
            fr["xr"][o] = (w, m)
            z = xs["n"] % len(XSp)
            xs["n"] += 1
            h = act.put(lambda: A.activation(XSp[z][:, 0, :], ps[:, :], ACT.Copy, scale=XS), m, xs["free"][z])
            c = act.put(lambda: A.copy(HT32[:, :], ps[:, :]), fr["ht"])
            lo = dve.put(lambda: V.scalar_tensor_tensor(out=XSp[z][:, 1, :], in0=ps[:, :], scalar=XS,
                                                        in1=XSp[z][:, 0, :], op0=ALU.mult, op1=ALU.subtract), h, c)
            tile_xs[l, i] = (z, lo)
            fr["ps"] = lo
            E = LAYERS[l]["E"]

            def lgm():
                for q in range(4):
                    m = nc.tensor.matmul(psl[:, 0:E], HT32[:, q * P:q * P + P], rw[l][:, q, :],
                                         start=(q == 0), stop=(q == 3))
                return m
            m = pe.put(lgm, c, lo, fr["pl"])
            fr["ht"] = m
            t = dve.put(lambda: V.tensor_copy(lg[:, i % 4, 0:E], psl[:, 0:E]), m, fr["lg"] if i % 4 == 0 else None)
            fr["pl"] = t
            lgt[l, i] = t
            return w

        rb = dict(mask=None, mac=None, wd={})
        wd_tok = {0: [None, None], 1: [None, None]}

        def bc(ap, shape):
            return ap.to_broadcast(shape)

        def route(l, b, psl):
            L = LAYERS[l]
            E, K = L["E"], L["K"]
            for q in range(4):
                t = lgt[l, 4 * b + q]
                a = dve.then(lambda q=q: V.max(mx[:, q, :], lg[:, q, 0:E]), t)
                dve.then(lambda q=q: V.max_index(ix[:, q, :], mx[:, q, :], lg[:, q, 0:E]), a)
            m0 = mx[:, :, 0:1]
            o = (OH[:, b * 64:b * 64 + 64] if l == 0 else OH[:, 0:4 * K * E]).rearrange("p (q k e) -> p q k e", q=4, k=K)
            ot = OT[:, 0:4 * K * E].rearrange("p (q k e) -> p q k e", q=4, k=K)
            a = dve.then(lambda: V.tensor_tensor(ex[:, :, 0:E], lg[:, :, 0:E], bc(m0, [P, 4, E]), ALU.subtract))
            c = dve.then(lambda: V.tensor_tensor(et[:, :, 0:K], mx[:, :, 0:K], bc(m0, [P, 4, K]), ALU.subtract))
            fr["lg"] = a
            a = act.put(lambda: A.activation(ex[:, :, 0:E], ex[:, :, 0:E], ACT.Exp), a)
            c = act.put(lambda: A.activation(et[:, :, 0:K], et[:, :, 0:K], ACT.Exp), c)
            x = dve.then(lambda: V.tensor_copy(ixf[:, :, 0:K], ix[:, :, 0:K]))
            x = dve.then(lambda: V.tensor_tensor(
                o, bc(iota[:, 0:E].unsqueeze(1).unsqueeze(1), [P, 4, K, E]),
                bc(ixf[:, :, 0:K].unsqueeze(3), [P, 4, K, E]), ALU.is_equal), x)
            mk = dve.then(lambda: V.tensor_reduce(mask[:, :, 0:E], o.rearrange("p q k e -> p q e k"), AX_X, ALU.add),
                         x, rb["mask"])
            a = dve.then(lambda: V.tensor_reduce(s1[:, :, :], ex[:, :, 0:E], AX_X, ALU.add), a)
            a = dve.then(lambda: V.reciprocal(s1[:, :, :], s1[:, :, :]), a)
            if l == 1:
                a = dve.then(lambda: V.tensor_scalar(s1[:, :, :], s1[:, :, :], UN, None, ALU.mult), a)
            a = dve.then(lambda: V.tensor_tensor(et[:, :, 0:K], et[:, :, 0:K], bc(s1[:, :, :], [P, 4, K]), ALU.mult), a, c)
            if l == 0:
                a = dve.then(lambda: V.tensor_reduce(s2[:, :, :], et[:, :, 0:K], AX_X, ALU.add), a)
                a = dve.then(lambda: V.reciprocal(s2[:, :, :], s2[:, :, :]), a)
                a = dve.then(lambda: V.tensor_scalar(s2[:, :, :], s2[:, :, :], UN, None, ALU.mult), a)
                a = dve.then(lambda: V.tensor_tensor(et[:, :, 0:K], et[:, :, 0:K], bc(s2[:, :, :], [P, 4, K]), ALU.mult), a)
            a = dve.then(lambda: V.tensor_tensor(ot, o, bc(et[:, :, 0:K].unsqueeze(3), [P, 4, K, E]), ALU.mult), a)
            a = dve.then(lambda: V.tensor_reduce(Wd[b % 2][:, :, 0:E], ot.rearrange("p q k e -> p q e k"), AX_X, ALU.add),
                        a, wd_tok[l][b % 2], wd_tok[0][b % 2])
            wd_tok[l][b % 2] = r_wd[l].start(sp, b % 2, lambda: S.dma_start(
                X[l][b * 512:b * 512 + 512, D:D + E].rearrange("(q p) e -> p q e", p=P), Wd[b % 2][:, :, 0:E]), a)
            n = dve.then(lambda: V.tensor_reduce(mred[:, 0:E], mask[:, :, 0:E].rearrange("p q e -> p e q"), AX_X, ALU.add), mk)
            if b == 0:
                n = dve.then(lambda: V.tensor_copy(macc[1][:, 0:E], mred[:, 0:E]), n, rb["mac"])
            else:
                n = dve.then(lambda: V.tensor_tensor(macc[b + 1][:, 0:E], macc[b][:, 0:E], mred[:, 0:E], ALU.add), n)

            def excl():
                for q in range(4):
                    outp = psl[:, q * E:q * E + E]
                    m = nc.tensor.matmul(outp, U16[:, :], mask[:, q, 0:E], start=True, stop=(q == 0 and b == 0))
                    for r in range(q):
                        m = nc.tensor.matmul(outp, ones16[:, :], mask[:, r, 0:E], start=False,
                                             stop=(r == q - 1 and b == 0))
                    if b:
                        m = nc.tensor.matmul(outp, ones16[:, :], macc[b][:, 0:E], start=False, stop=True)
                return m
            m = pe.put(excl, mk, n, t_c16, fr["pl"], fr["ps"])
            rb["mask"] = m
            rb["mac"] = m
            if l == 0:
                pb = posb[:, b * 32:b * 32 + 32]
                t = dve.then(lambda: V.tensor_copy(pb, psl[:, 0:32]), m)
                fr["pl"] = t
                return
            t = dve.then(lambda: V.tensor_tensor(
                ot, o, bc(psl[:, 0:4 * E].rearrange("p (q e) -> p q e", q=4).unsqueeze(2), [P, 4, K, E]), ALU.mult), m, a)
            fr["pl"] = t
            ks = slice(b * 4 * K, (b + 1) * 4 * K)
            t = dve.then(lambda: V.tensor_reduce(gq[:, ks].rearrange("p (q k) -> p q k", q=4), ot, AX_X, ALU.add), t)
            t = split_slot(ks, t)
            t = dve.then(lambda: V.scalar_tensor_tensor(out=ja[:, ks].rearrange("p (q k) -> p q k", q=4),
                                                       in0=ixf[:, :, 0:K], scalar=4.0,
                                                       in1=gj[:, ks].rearrange("p (q k) -> p q k", q=4),
                                                       op0=ALU.mult, op1=ALU.add), t)
            t = dve.then(lambda: V.tensor_scalar(gj[:, ks], gq[:, ks], float(CAP), -1000.0, ALU.is_ge, ALU.mult), t)
            return dve.then(lambda: V.tensor_tensor(qa[:, ks], qa[:, ks], gj[:, ks], ALU.add), t)

        def split_slot(ks, t):
            t = dve.then(lambda: V.tensor_copy(gi[:, ks], gq[:, ks]), t)
            t = dve.then(lambda: V.tensor_single_scalar(gi[:, ks], gi[:, ks], 7, ALU.arith_shift_right), t)
            t = dve.then(lambda: V.tensor_copy(gj[:, ks], gi[:, ks]), t)
            return dve.then(lambda: V.scalar_tensor_tensor(out=qa[:, ks], in0=gj[:, ks], scalar=-128.0, in1=gq[:, ks],
                                                          op0=ALU.mult, op1=ALU.add), t)

        def starts0(psl):
            m = pe.put(lambda: nc.tensor.matmul(psl[:, 0:8], ones16[:, :], macc[4][:, 0:8], start=True, stop=True),
                       fr["pl"], rb["mac"], (dve.sem, dve.n))
            rb["mac"] = m
            t = dve.then(lambda: V.tensor_scalar(cni[:, :], psl[:, 0:8], 127.0, None, ALU.add), m)
            fr["pl"] = t
            t = dve.then(lambda: V.tensor_single_scalar(cni[:, :], cni[:, :], 7, ALU.arith_shift_right), t)
            t = dve.then(lambda: V.tensor_copy(cn[:, 0, :], cni[:, :]), t)
            t = dve.then(lambda: V.tensor_tensor_scan(cn[:, 1, :], ones[:, :], cn[:, 0, :], 0.0, ALU.mult, ALU.add), t)
            t = dve.then(lambda: V.tensor_tensor(cn[:, 2, :], cn[:, 1, :], cn[:, 0, :], ALU.subtract), t)
            t = dve.then(lambda: V.tensor_scalar(cn[:, 2, :], cn[:, 2, :], 128.0, None, ALU.mult), t)
            pv = posb[:, :].rearrange("p (i e) -> p i e", i=16)
            ov = OH[:, 0:256].rearrange("p (i k e) -> p i k e", i=16, k=2)
            t = dve.then(lambda: V.tensor_tensor(pv, pv, bc(cn[:, 2:3, :], [P, 16, 8]), ALU.add), t)
            t = dve.then(lambda: V.tensor_tensor(ov, ov, bc(pv.unsqueeze(2), [P, 16, 2, 8]), ALU.mult), t)
            ks = slice(0, 32)
            t = dve.then(lambda: V.tensor_reduce(gq[:, ks].rearrange("p (i k) -> p i k", i=16), ov, AX_X, ALU.add), t)
            t = split_slot(ks, t)
            t = dve.then(lambda: V.tensor_copy(ja[:, ks], gj[:, ks]), t)
            u = dve.then(lambda: V.tensor_tensor(ohB[:, :, :], bc(cn[:, 1:2, :], [P, 39, 8]),
                                                bc(iota[:, 0:39].unsqueeze(2), [P, 39, 8]), ALU.is_le))
            u = dve.then(lambda: V.tensor_reduce(ebf[:, :].unsqueeze(2), ohB[:, :, :], AX_X, ALU.add), u)
            u = dve.then(lambda: V.tensor_scalar(ebf[:, :], ebf[:, :], 7.0, None, ALU.min), u)
            dve.then(lambda: V.tensor_copy(ebi, ebf[:, :]), u)
            u = dve.then(lambda: V.tensor_tensor(ohB[:, :, :], bc(iota[:, 0:8].unsqueeze(1), [P, 39, 8]),
                                                bc(ebf[:, :].unsqueeze(2), [P, 39, 8]), ALU.is_equal), u)
            return u

        def tables(l, psl, t):
            L = LAYERS[l]
            K, NB = L["K"], L["NB"]
            free = [None, None]
            for g in range(4 * K):
                s = g % 2
                for r in range(4):
                    n = 4 * g + r
                    i = n // K
                    dve.put(lambda s=s, r=r, n=n: V.tensor_scalar(A16[s][:, r, :], iota16[:, :], qa[:, n:n + 1], None,
                                                                  ALU.is_equal), t, free[s])
                    d = dve.put(lambda s=s, r=r, n=n, i=i: V.tensor_scalar(
                        B16[s][:, r, 0:NB], iota16[:, 0:NB], ja[:, n:n + 1], tid[:, i:i + 1], ALU.is_equal, ALU.mult))

                def mm(g=g, s=s):
                    for r in range(4):
                        m = nc.tensor.matmul(psl[:, 0:NB], A16[s][:, r, :], B16[s][:, r, 0:NB],
                                             start=(g == 0 and r == 0), stop=(g == 4 * K - 1 and r == 3))
                    return m
                free[s] = pe.put(mm, d, fr["pl"], fr["ps"])
            m = free[(4 * K - 1) % 2]
            rb["tab"] = m
            t = dve.put(lambda: V.scalar_tensor_tensor(out=idf[:, 0:NB], in0=psl[:, 0:NB], scalar=0.0,
                                                       in1=dconst[:, 0:NB], op0=ALU.is_equal, op1=ALU.mult), m)
            t = dve.put(lambda: V.scalar_tensor_tensor(out=idx[l][:, 0:NB], in0=psl[:, 0:NB], scalar=-1.0,
                                                       in1=idf[:, 0:NB], op0=ALU.add, op1=ALU.add), t)
            fr["pl"] = t
            return t

        wt = dict(n=0, free=[None] * 2)

        def wload(src, dst, pieces, *after):
            out = []
            for c0, cw in pieces:
                s = wt["n"] % 2
                wt["n"] += 1
                t = r_st.start(sp, s, lambda s=s, c0=c0, cw=cw: S.dma_start(ST[s][:, 0:cw], src[:, c0:c0 + cw]),
                               wt["free"][s])
                hi = Whi[:, dst + c0:dst + c0 + cw]
                lo = Wlo[:, dst + c0:dst + c0 + cw]
                a = act.put(lambda s=s, cw=cw: A.activation(ST[s][:, 0:cw], ST[s][:, 0:cw], ACT.Copy, scale=WS), t)
                a = act.put(lambda s=s, cw=cw, hi=hi: A.copy(hi, ST[s][:, 0:cw]), a, *after)
                a = pool.put(lambda s=s, cw=cw, hi=hi, lo=lo: G.tensor_tensor(lo, ST[s][:, 0:cw], hi, ALU.subtract),
                             a, *after)
                wt["free"][s] = a
                out.append(a)
            return out

        blocks = []
        st = dict(g=0, h=[None, None], hs=[None, None], o=[None, None], ob=[None] * 4, sg=None,
                  gf=[None, None], chain=[], last=None, xg=[None] * 3, px=None, ph=None, lo=0, wkps=None)

        def gather(n):
            if n >= len(blocks) or blocks[n]["kind"] != "routed" or "g" in blocks[n]:
                return
            B = blocks[n]
            l, j = B["l"], B["j"]
            s = st["g"] % 3
            st["g"] += 1
            w = D + LAYERS[l]["E"]
            B["xg"] = s
            B["g"] = r_g.start(pool, s, lambda: G.indirect_dma_start(
                out=XG[s][:, 0:w], out_offset=None, in_=X[l][:, :],
                in_offset=bass.IndirectOffsetOnAxis(ap=idx[l][:, j:j + 1], axis=0)), B["ready"], t_dummy, *B["rows"],
                *(st["xg"][s] or ()))

        def turn(n):
            if n >= len(blocks) or blocks[n]["kind"] != "routed":
                return
            B = blocks[n]
            l, s, j = B["l"], B["xg"], B["j"]
            w = WSL[:, n % 8:n % 8 + 1]

            def tr():
                for q in range(4):
                    m = nc.tensor.transpose(psX[:, q * P:q * P + P], XG[s][:, q * P:q * P + P], ident)
                return m
            m = pe.put(tr, B["g"], st["px"], fr["ps"], fr["pl"], st["wkps"])
            if l == 0:
                u = dve.put(lambda: V.tensor_tensor_reduce(jnk[:, :], XG[s][:, D:D + 8], ohB[:, j, :], 1.0, 0.0,
                                                           ALU.mult, ALU.add, w), B["g"], st.get("u"))
            else:
                e = j // 4
                u = dve.put(lambda: V.tensor_copy(w, XG[s][:, D + e:D + e + 1]), B["g"])
            st["u"] = u
            B["u"] = u
            st["xg"][s] = (m, u)
            z = xs["n"] % len(XSp)
            xs["n"] += 1
            h = act.put(lambda: A.activation(XSp[z][:, 0, :], psX[:, :], ACT.Copy, scale=XS), m, xs["free"][z])
            lo = dve.put(lambda: V.scalar_tensor_tensor(out=XSp[z][:, 1, :], in0=psX[:, :], scalar=XS,
                                                        in1=XSp[z][:, 0, :], op0=ALU.mult, op1=ALU.subtract), h)
            st["px"] = lo
            B["xs"] = (z, lo)

        def gu(n):
            B = blocks[n]
            l = B["l"]
            F = LAYERS[l]["F"]
            z, t = B["xs"]
            a = n % 2
            hx = XSp[z]

            def mm():
                if B.get("reg"):
                    j = B["j"]
                    r = nc.tensor.value_load(ebi[0:1, j:j + 1], min_val=0, max_val=7)
                    B["rv"] = r

                    def w(half, off, n):
                        return half[:, bass.ds(r * 3072 + off, n)]
                else:
                    def w(half, off, n):
                        return half[:, B["w"] + off:B["w"] + off + n]
                B["wf"] = w
                if l == 0:
                    outs = [(psG[a][0][:, 0:512], 0, 512)]
                else:
                    outs = [(psG[a][0][:, 0:F], 0, F), (psG[a][1][:, 0:F], F, F)]
                for q in range(4):
                    off = q * 2 * F
                    for x, half in ((0, Whi), (0, Wlo), (1, Whi)):
                        first, last = q == 0 and x == 0 and half is Whi, q == 3 and x == 1
                        for o, c, nn in outs:
                            m = nc.tensor.matmul(o, hx[:, x, q * P:q * P + P], w(half, off + c, nn),
                                                 start=first, stop=last)
                return m
            m = pe.put(mm, t, st["gf"][a], *B["wt"])
            B["gu"] = m
            if B.get("endx", True):
                xs["free"][z] = m
            g, u = (psG[a][0][:, 0:F], psG[a][0][:, F:2 * F]) if l == 0 else (psG[a][0][:, 0:F], psG[a][1][:, 0:F])
            s = act.put(lambda: A.activation(H32[a][:, 0:F], g, ACT.Silu, scale=UN), m, st["h"][a])
            h = dve.put(lambda: V.scalar_tensor_tensor(out=H32[a][:, 0:F], in0=u, scalar=XS * UN, in1=H32[a][:, 0:F],
                                                       op0=ALU.mult, op1=ALU.mult), s)
            st["gf"][a] = h
            B["h"] = h

        def hturn(n):
            B = blocks[n]
            a = n % 2
            NK = LAYERS[B["l"]]["NK"]

            def tr():
                for q in range(NK):
                    m = nc.tensor.transpose(psH[:, q * P:q * P + P], H32[a][:, q * P:q * P + P], ident)
                return m
            m = pe.put(tr, B["h"], st["ph"])
            st["h"][a] = m
            w = NK * P
            h = act.put(lambda: A.copy(HS[a][:, 0, 0:w], psH[:, 0:w]), m, st["hs"][a])
            lo = dve.put(lambda: V.tensor_tensor(HS[a][:, 1, 0:w], psH[:, 0:w], HS[a][:, 0, 0:w], ALU.subtract), h)
            st["ph"] = lo
            B["hs"] = lo

        def down(n):
            B = blocks[n]
            l, a = B["l"], n % 2
            L = LAYERS[l]
            NK = L["NK"]
            o = B["o"] % 2
            off0 = 8 * L["F"]

            def mm():
                for q in range(NK):
                    for x, half in ((0, Whi), (0, Wlo), (1, Whi)):
                        m = nc.tensor.matmul(psO[o][:, :], HS[a][:, x, q * P:q * P + P],
                                             B["wf"](half, off0 + q * 512, 512),
                                             start=(q == 0 and x == 0 and half is Whi and B["first"]),
                                             stop=(q == NK - 1 and x == 1 and B["last"]))
                return m
            m = pe.put(mm, B["hs"], st["o"][o] if B["first"] else None)
            st["hs"][a] = m
            B["done"] = m
            st["done"] = m
            if not B["last"]:
                return
            k = B["o"] % 4
            if B["kind"] == "shared":
                s, _ = tile_x[l, B["i"]]
                i = B["i"]
                t = dve.put(lambda: V.scalar_tensor_tensor(out=OB[k][:, :], in0=psO[o][:, :], scalar=UN,
                                                           in1=XT[s][:, :], op0=ALU.mult, op1=ALU.add), m, st["ob"][k])
                xt["free"][s] = t
                w = r_y.start(sp, k, lambda: S.dma_start(Y[l][i * P:i * P + P, :], OB[k][:, :]), t)
                st["chain"].append(w)
            else:
                j = B["j"]
                t = act.put(lambda: A.activation(OB[k][:, :], psO[o][:, :], ACT.Copy,
                                                 scale=WSL[:, n % 8:n % 8 + 1]), m, B["u"], st["ob"][k])
                if l == 0 or j % 4 == 0:
                    st["cur"] = st["chain"]
                    st["chain"] = []
                w = r_o.start(pool, k, lambda: G.indirect_dma_start(
                    out=Y[l][:, :], out_offset=bass.IndirectOffsetOnAxis(ap=idx[l][:, j:j + 1], axis=0),
                    in_=OB[k][:, :], in_offset=None, compute_op=ALU.add), t, t_dummy, *st["cur"])
                st["chain"].append(w)
            st["o"][o] = t
            st["ob"][k] = w

        def step(n):
            gather(n + 3)
            turn(n + 1)
            gu(n)
            rest(n)

        def rest(n):
            if n - 1 >= st["lo"]:
                hturn(n - 1)
            if n - 2 >= st["lo"]:
                down(n - 2)

        def flush():
            n = len(blocks)
            hturn(n - 1)
            down(n - 2)
            down(n - 1)
            st["lo"] = n

        no = [0]

        def add(**kw):
            kw.setdefault("first", True)
            kw.setdefault("last", True)
            kw["o"] = no[0]
            if kw["last"]:
                no[0] += 1
            blocks.append(kw)
            return len(blocks) - 1

        PXF, PLG = psG[0][1], psG[1][1]
        wsh = wload(W0[8], 7 * 3072, WCH[0])
        for c in range(4):
            wkv(0, 0, c, psX, None)
        load_x(0, 0)
        wl = [(e, c) for e in range(7) for c in WCH[0]]
        w0 = []
        xrows = []
        for i in range(NT):
            b, q = divmod(i, 4)
            if b < 3:
                wkv(0, b + 1, q, psX, None)
            if i + 1 < NT:
                load_x(0, i + 1)
            h, e = RTready[0, b]
            xrows.append(front(0, i, RT[h][:, q, :], e, PXF, PLG))
            if q == 3:
                RTfree[h] = [fr["bs"]]
                route(0, b, PLG)
            n = add(kind="shared", l=0, i=i, xs=tile_xs[0, i], w=7 * 3072, wt=[wsh[-1]])
            gu(n)
            rest(n)
            for e, c in wl[:2] if i else wl[:1]:
                w0 += wload(W0[e], e * 3072, [c])
            wl = wl[2 if i else 1:]
        flush()
        for e, c in wl:
            w0 += wload(W0[e], e * 3072, [c])
        w0 += wload(W0[7], 7 * 3072, WCH[0], st["done"])
        u = starts0(PLG)
        tab = tables(0, PLG, u)
        RTfree[1] = RTfree[1] + [rb["tab"]]
        base = len(blocks)
        for j in range(39):
            add(kind="routed", l=0, j=j, reg=True, ready=tab, rows=xrows[-2:] + wd_tok[0], wt=[w0[-1], u])
        for n in (base, base + 1, base + 2):
            gather(n)
        st["wkps"] = wk["psfree"]
        turn(base)
        rt1w = None
        todo = [(b, c) for b in range(4) for c in range(4)]
        for n in range(base, base + 39):
            if todo and (n - base) % 7 in (0, 2, 4):
                rt1w = wkv(1, *todo.pop(0), PXF, fr["ps"]) or rt1w
            step(n)
        while todo:
            rt1w = wkv(1, *todo.pop(0), PXF, fr["ps"]) or rt1w
        flush()
        end0 = st["done"]
        done0 = list(st["chain"])

        st["chain"] = []
        order = [32, 33] + list(range(32))
        slot = {e: (m % 5) * 4352 for m, e in enumerate(order)}
        wtok, last_use = {}, {}

        def load1(m, piece):
            e = order[m]
            after = end0 if m < 5 else last_use[order[m - 5]]
            wtok[e] = wload(W1[e], slot[e], [WCH[1][piece]], after)[-1]

        for m in range(2):
            for c in range(4):
                load1(m, c)
        fr["ps"] = st["px"]
        rt_free = [RTfree[h] + [RTready[1, 2 + h][1]] for h in range(2)]
        rt_tok = {}

        def load_rt(b):
            h = b % 2
            rt_tok[b] = r_rtl.start(sp, h, lambda: S.dma_start(
                RT[h][:, :, :], RT1[b * 512:b * 512 + 512, :].rearrange("(q p) c -> p q c", p=P)), rt1w, *rt_free[h])

        load_rt(0)
        load_rt(1)
        load_x(1, 0, *done0)
        load_x(1, 1, *done0)
        xrows = []
        for i in range(NT + 1):
            if i < NT:
                b, q = divmod(i, 4)
                if i >= 2:
                    load_x(1, i)
                xrows.append(front(1, i, RT[b % 2][:, q, :], rt_tok[b], psX, psX))
                if q == 3:
                    rt_free[b % 2] = [fr["bs"]]
                    if b < 2:
                        load_rt(b + 2)
                    t = route(1, b, psX)
                    if b == 3:
                        tab = tables(1, psX, t)
            if i >= 1:
                for hf in range(2):
                    n = add(kind="shared", l=1, i=i - 1, xs=tile_xs[1, i - 1], w=slot[32 + hf], wt=[wtok[32 + hf]],
                            first=(hf == 0), last=(hf == 1), endx=(hf == 1))
                    gu(n)
                    rest(n)
                if i <= 12:
                    load1(2 + (i - 1) // 4, (i - 1) % 4)
        base = len(blocks)
        for j in range(128):
            add(kind="routed", l=1, j=j, ready=tab, rows=xrows[-2:] + wd_tok[1], w=slot[j // 4])
        for n in (base, base + 1, base + 2):
            gather(n)
        turn(base)
        for g in range(128):
            n = base + g
            blocks[n]["wt"] = [wtok[g // 4]]
            step(n)
            if g == 2:
                last_use[32] = last_use[33] = blocks[base - 1]["done"]
            if g % 4 == 2 and g > 4:
                last_use[g // 4 - 1] = blocks[base + g - 3]["done"]
            if 3 <= g < 7:
                for c in (2 * (g - 3), 2 * (g - 3) + 1):
                    load1(5 + c // 4, c % 4)
            elif g >= 7 and 7 + (g - 7) // 4 < 34:
                load1(7 + (g - 7) // 4, (g - 7) % 4)
        flush()
        last = [(r_o.sems[k], r_o.v[k]) for k in range(4)] + [(r_y.sems[k], r_y.v[k]) for k in range(4)]
        sp.wait(last)

        block = ctx.enter_context(nc.Block())

        @block.sync
        def _(eng):
            sp.run(eng)

        @block.gpsimd
        def _(eng):
            pool.run(eng)

        @block.scalar
        def _(eng):
            act.run(eng)

        @block.vector
        def _(eng):
            dve.run(eng)

        @block.tensor
        def _(eng):
            pe.run(eng)


def kernel(**inputs):
    import numpy as np
    import concourse.bacc as bacc
    from concourse.bass_utils import run_bass_kernel_spmd

    f = {k: np.asarray(v) for k, v in inputs.items()}
    x = np.ascontiguousarray(f["x"].reshape(2048, 512))
    fT = np.ascontiguousarray(f["fside_BxSxS_0"].reshape(2048, 512).T)
    cst = np.zeros((128, 528), np.float32)
    p = np.arange(128)
    cst[:, 0:128] = np.eye(128)
    cst[:, 128:256] = p[None, :]
    cst[:, 256:384] = p[:, None] < p[None, :]
    cst[:, 384:512] = 2049 + 128 * (p[None, :] % 4) + p[:, None]
    cst[:, 512:528] = 128 * np.arange(16)[None, :] + p[:, None] + 1

    def cols(v):
        return v.reshape(4, 128).T

    svec = np.ascontiguousarray(np.concatenate(
        [cols(f[n]) for n in ("L0_cond_w", "L1_cond_w", "L0_cond_u", "L1_cond_u")], axis=1))
    cond = np.ascontiguousarray(np.broadcast_to(f["cond_512"][None], (128, 4, 128)))
    rms = np.ascontiguousarray(np.broadcast_to(f["L0_ffn_rms_weight"][None], (128, 512)))
    rout = np.ascontiguousarray(f["L0_ffn_router_w"].reshape(4, 128, 8).transpose(1, 0, 2))
    gatew = np.ascontiguousarray(f["L1_ffn_gate_w"].T.reshape(4, 128, 32).transpose(1, 0, 2))

    def pack(gate, up, downw, nk):
        e, _, F = gate.shape
        gu = np.concatenate([gate, up], axis=2).reshape(e, 4, 128, 2 * F).transpose(0, 2, 1, 3).reshape(e, 128, 8 * F)
        dp = np.zeros((e, nk * 128, 512), np.float32)
        dp[:, :F] = downw
        dp = dp.reshape(e, nk, 128, 512).transpose(0, 2, 1, 3).reshape(e, 128, nk * 512)
        return np.ascontiguousarray(np.concatenate([gu, dp], axis=2))

    W0 = pack(np.concatenate([f["L0_ffn_w_gate"], f["L0_ffn_sw_gate"][None]]),
              np.concatenate([f["L0_ffn_w_up"], f["L0_ffn_sw_up"][None]]),
              np.concatenate([f["L0_ffn_w_down"], f["L0_ffn_sw_down"][None]]), 2)

    def halves(a):
        return a.reshape(512, 2, 352).transpose(1, 0, 2)

    W1 = pack(np.concatenate([f["L1_ffn_w1"], halves(f["L1_ffn_sw1"])]),
              np.concatenate([f["L1_ffn_w3"], halves(f["L1_ffn_sw3"])]),
              np.concatenate([f["L1_ffn_w2"], f["L1_ffn_sw2"].reshape(2, 352, 512)]), 3)

    nc = bacc.Bacc("TRN2", target_bir_lowering=False, num_devices=1)
    arrays, args = {}, []
    for name, a in (("x", x), ("fT", fT), ("cst", cst), ("svec", svec), ("cond", cond), ("rms", rms),
                    ("rout", rout), ("gatew", gatew), ("W0", W0), ("W1", W1)):
        arrays[name] = a
        args.append(nc.dram_tensor(name, list(a.shape), mybir.dt.from_np(a.dtype), kind="ExternalInput").ap())
    out = nc.dram_tensor("out", [ROWS, D], F32, kind="ExternalOutput").ap()
    build(nc, *args, out)
    r = run_bass_kernel_spmd(nc, [arrays], core_ids=[0])
    return r.results[0]["out"][:2048].reshape(4, 512, 512)
```

```python
from contextlib import ExitStack

import concourse.bass as bass
from concourse import mybir

P = 128
T = 2048
D = 512
NT = T // P
ROWS = T + 512
CAP = 512
F32 = mybir.dt.float32
F16 = mybir.dt.float16
I32 = mybir.dt.int32
U32 = mybir.dt.uint32
ALU = mybir.AluOpType
ACT = mybir.ActivationFunctionType
AX_X = mybir.AxisListType.X

XS = 8.0
WS = 64.0
UN = 1.0 / (XS * WS)

LAYERS = (
    dict(E=8, K=2, F=256, NK=2, NB=39, W=3072),
    dict(E=32, K=6, F=352, NK=3, NB=128, W=4352),
)
WCH = (((0, 1024), (1024, 1024), (2048, 1024)), ((0, 1088), (1088, 1088), (2176, 1088), (3264, 1088)))


class Line:

    def __init__(self, sem):
        self.sem, self.n, self.todo, self.seen = sem, 0, [], {}

    def wait(self, after):
        for tok in after:
            if tok is None:
                continue
            sem, v = tok
            if self.seen.get(id(sem), 0) < v:
                self.seen[id(sem)] = v
                self.todo.append((0, sem, v))

    def put(self, fn, *after):
        self.wait(after)
        self.n += 1
        self.todo.append((1, fn, (self.sem, 1)))
        return self.sem, self.n

    def then(self, fn, *after):
        return self.put(fn, (self.sem, self.n) if self.n else None, *after)

    def run(self, eng):
        for kind, a, b in self.todo:
            if kind == 0:
                eng.wait_ge(a, b)
            elif kind == 2:
                a()
            else:
                a().then_inc(*b)


class Ring:

    def __init__(self, sems):
        self.sems, self.v = sems, [0] * len(sems)

    def start(self, line, slot, fn, *after):
        line.wait(after)
        self.v[slot] += 16
        line.todo.append((1, fn, (self.sems[slot], 16)))
        return self.sems[slot], self.v[slot]


class Bank:

    def __init__(self, t):
        self.t, self.tok, self.busy = t, None, False

    def take(self):
        while self.busy:
            yield
        self.busy = True

    def give(self, tok):
        self.tok, self.busy = tok, False


class Tasks:

    def __init__(self):
        self.live = []

    def start(self, gen):
        self.live.append(gen)

    def turn(self):
        for g in list(self.live):
            if next(g, self) is self:
                self.live.remove(g)


E30 = 10686474581524.463


def build(nc, xtok, fT, cst, svec, cond, rms, rout, gatew, W0, W1, Y1):
    with ExitStack() as ctx:
        ctx.enter_context(nc.allow_low_precision(reason="sums of at most 16 ones are exact in float16"))

        def sb(name, shape, dt=F32):
            return ctx.enter_context(nc.sbuf_tensor(name, shape, dt))

        def sem(name):
            return ctx.enter_context(nc.semaphore(name))

        def ring(name, n):
            return Ring([sem(f"{name}{i}") for i in range(n)])

        X = [nc.dram_tensor(f"xrows{l}", [ROWS, D + LAYERS[l]["E"]], F32, kind="Internal").ap() for l in range(2)]
        Y0 = nc.dram_tensor("y0rows", [ROWS, D], F32, kind="Internal").ap()
        Y = [Y0, Y1]

        psG = [[ctx.enter_context(nc.psum_tensor(f"psG{a}{c}", [P, 512], F32)) for c in range(2)] for a in range(2)]
        psX = ctx.enter_context(nc.psum_tensor("psX", [P, 512], F32))
        psH = ctx.enter_context(nc.psum_tensor("psH", [P, 512], F32))
        psO = [ctx.enter_context(nc.psum_tensor(f"psO{a}", [P, 512], F32)) for a in range(2)]

        C = sb("C", [P, 528])
        ident, iota, U32f, dconst, tid = C[:, 0:128], C[:, 128:256], C[:, 256:384], C[:, 384:512], C[:, 512:528]
        iota16 = sb("iota16", [P, 128], F16)
        U16 = sb("U16", [P, 128], F16)
        ones16 = sb("ones16", [P, 128], F16)
        ones = sb("ones", [P, 8])
        half = sb("half", [P, 1])
        sv = sb("sv", [P, 16])
        rmsb = sb("rmsb", [P, D])
        rw = [sb("rw0", [P, 4, 8]), sb("rw1", [P, 4, 32])]
        dec = sb("dec", [P, 2, 4, 4])
        cs = sb("cs", [P, 8, 8])

        Whi = sb("Whi", [P, 8 * 3072], F16)
        Wlo = sb("Wlo", [P, 8 * 3072], F16)
        ST = [sb(f"ST{i}", [P, 1088]) for i in range(2)]

        WK = [{n: sb(f"wk{n}{i}", [P, 512]) for n in ("K", "EK", "EU", "EKV", "NF", "DF")} for i in range(2)]
        RT = [sb(f"RT{i}", [P, 4, 512]) for i in range(2)]
        XT = [sb(f"XT{i}", [P, 512]) for i in range(4)]
        BS = sb("BS", [P, 512])
        XR = [sb(f"XR{i}", [P, 512]) for i in range(2)]
        HT32 = sb("HT32", [P, 512])
        cnd = HT32[:, :].rearrange("p (b k) -> p b k", b=4)
        sm = sb("sm", [P, NT, 4])
        XSp = [sb(f"XSp{i}", [P, 2, 512], F16) for i in range(4)]
        XG = [sb(f"XG{i}", [P, D + 32]) for i in range(3)]
        zero = XG[0]
        WSL = sb("WSL", [P, 8])
        jnk = sb("jnk", [P, 8])
        H32 = [sb(f"H32{i}", [P, 384]) for i in range(2)]
        HS = [sb(f"HS{i}", [P, 2, 384], F16) for i in range(2)]
        OB = [sb(f"OB{i}", [P, 512]) for i in range(4)]

        lg = sb("lg", [P, 4, 32])
        mx = sb("mx", [P, 4, 8])
        ix = sb("ix", [P, 4, 8], U32)
        ixf = sb("ixf", [P, 4, 8])
        ex = sb("ex", [P, 4, 32])
        et = sb("et", [P, 4, 8])
        s1 = sb("s1", [P, 4, 1])
        s2 = sb("s2", [P, 4, 1])
        OH = sb("OH", [P, 4 * 6 * 32])
        OT = sb("OT", [P, 4 * 6 * 32])
        mask = sb("mask", [P, 4, 32], F16)
        mred = sb("mred", [P, 32], F16)
        macc = [sb(f"macc{i}", [P, 32], F16) for i in range(5)]
        Wd = [sb(f"Wd{i}", [P, 4, 32]) for i in range(2)]
        posb = sb("posb", [P, 16 * 8])
        gq = sb("gq", [P, 96])
        gi = sb("gi", [P, 96], I32)
        gj = sb("gj", [P, 96])
        qa = sb("qa", [P, 96])
        ja = sb("ja", [P, 96])
        cn = sb("cn", [P, 4, 8])
        cni = sb("cni", [P, 8], I32)
        ebf = sb("ebf", [P, 39])
        ebi = gi[:, 48:87]
        ohB = sb("ohB", [P, 39, 8], F16)
        AB = [RT[1][:, i, :].bitcast(F16).rearrange("p (a r n) -> p a r n", a=2, r=4) for i in range(2)]
        A16, B16 = [v[:, 0] for v in AB], [v[:, 1] for v in AB]
        idf = U32f
        idx = [sb("idx0", [P, 39], U32), posb[:, :].bitcast(U32)]

        pe, act, dve, pool, sp = (Line(sem(n)) for n in ("s_pe", "s_act", "s_dve", "s_pool", "s_sp"))
        s_c, s_z = ring("s_c", 1), ring("s_z", 1)
        r_k, r_x, r_st, r_g, r_o = ring("r_k", 2), ring("r_x", 4), ring("r_st", 2), ring("r_g", 3), ring("r_o", 4)
        r_y = ring("r_y", 4)
        r_xr = [ring("r_xr0", 2), ring("r_xr1", 2)]
        r_wd = [ring("r_wd0", 2), ring("r_wd1", 2)]
        V, A, G = nc.vector, nc.scalar, nc.gpsimd
        S = nc.sync

        for dst, src in ((C[:, :], cst), (sv[:, :], svec), (cnd[:, :, :], cond), (rmsb[:, :], rms),
                         (rw[0][:, :, :], rout), (rw[1][:, :, :], gatew)):
            t_c = s_c.start(sp, 0, lambda d=dst, s=src: S.dma_start(d, s))
        t_z = dve.put(lambda: V.memset(zero[:, :], 0.0))
        dve.put(lambda: V.memset(ones16[:, :], 1.0))
        dve.put(lambda: V.memset(ones[:, :], 1.0))
        t_half = dve.put(lambda: V.memset(half[:, :], -0.5))
        for h in H32:
            dve.put(lambda h=h: V.memset(h[:, :], 0.0))
        dve.put(lambda: V.tensor_copy(iota16[:, :], iota), t_c)
        t_c16 = dve.put(lambda: V.tensor_copy(U16[:, :], U32f))
        for k in range(4):
            rows = slice(T + P * k, T + P * k + P)
            for dst, w in ((X[0], D + 8), (X[1], D + 32), (Y[0], D), (Y[1], D)):
                t_dummy = s_z.start(sp, 0, lambda d=dst, r=rows, w=w: S.dma_start(d[r, :], zero[:, 0:w]), t_z)

        t = dve.then(lambda: V.tensor_reduce(cs[:, 0, 0:4], cnd[:, :, :], AX_X, ALU.add), t_c)
        t = act.put(lambda: A.activation(cs[:, 1, 0:4], cs[:, 0, 0:4], ACT.Exp, scale=-1.0), t)
        t = dve.then(lambda: V.tensor_scalar(cs[:, 2, 0:4], cs[:, 1, 0:4], 1.0, None, ALU.add), t)
        t = dve.then(lambda: V.reciprocal(cs[:, 3, 0:4], cs[:, 2, 0:4]), t)
        dve.then(lambda: V.tensor_scalar(cs[:, 4, 0:4], cs[:, 3, 0:4], 0.5, 0.5, ALU.mult, ALU.add), t)
        t_cs = dve.then(lambda: V.tensor_scalar(cs[:, 5, 0:4], cs[:, 3, 0:4], 0.1, 0.4, ALU.mult, ALU.add))
        t = act.put(lambda: A.activation(cs[:, 6, :], sv[:, 0:8], ACT.Exp), t_c)
        t_w = act.put(lambda: A.activation(cs[:, 7, :], cs[:, 6, :], ACT.Exp, scale=-1.0), t)
        for l in range(2):
            for c in range(4):
                t_dec = dve.then(lambda l=l, c=c: V.tensor_scalar(dec[:, l, c, :], cs[:, 4, 0:4],
                                                                 cs[:, 7, 4 * l + c:4 * l + c + 1], None, ALU.mult),
                                t_w, t_cs)

        wk = dict(n=0, done=0, free=[None, None], kfree=[None, None])
        rt_ready, rt_free = {}, {(0, 0): [], (0, 1): []}

        def wkv(l, b, c, bank):
            n = wk["n"]
            wk["n"] += 1
            s = n % 2
            B = WK[s]
            k = B["K"]
            t_k = r_k.start(sp, s, lambda: S.dma_start(k[:, :], fT[c * P:c * P + P, b * 512:b * 512 + 512]),
                            wk["kfree"][s])
            u = sv[:, 8 + 4 * l + c:9 + 4 * l + c]
            dc = dec[:, l, c, b:b + 1].to_broadcast([P, 512])
            yield
            a0 = dve.put(lambda: V.tensor_scalar(B["EK"][:, :], k[:, :], 30.0, None, ALU.min), t_k, wk["free"][s])
            e1 = act.put(lambda: A.activation(B["EU"][:, :], k[:, :], ACT.Exp, bias=u), t_k, t_c, wk["free"][s])
            e0 = act.put(lambda: A.activation(B["EK"][:, :], B["EK"][:, :], ACT.Exp), a0)
            yield
            p0 = pool.put(lambda: G.tensor_tensor(B["EKV"][:, :], B["EK"][:, :], k[:, :], ALU.mult), e0, wk["free"][s])
            p1 = dve.put(lambda: V.scalar_tensor_tensor(out=B["EU"][:, :], in0=B["EU"][:, :], scalar=E30,
                                                        in1=B["EK"][:, :], op0=ALU.min, op1=ALU.subtract), e0, e1)
            p2 = pool.put(lambda: G.tensor_tensor(k[:, :], B["EU"][:, :], k[:, :], ALU.mult), p1, p0)
            yield
            dve.put(lambda: V.tensor_tensor_scan(B["DF"][:, :], dc, B["EK"][:, :], 0.0, ALU.mult, ALU.add), e0, t_dec)
            d1 = dve.then(lambda: V.tensor_tensor_scan(B["EK"][:, ::-1], dc, B["EK"][:, ::-1], 0.0, ALU.mult, ALU.add), p0)
            t1 = pool.put(lambda: G.tensor_tensor(B["DF"][:, :], B["DF"][:, :], B["EK"][:, :], ALU.add), d1)
            t2 = pool.put(lambda: G.tensor_tensor(B["DF"][:, :], B["DF"][:, :], B["EU"][:, :], ALU.add), t1)
            yield
            dve.put(lambda: V.tensor_tensor_scan(B["NF"][:, :], dc, B["EKV"][:, :], 0.0, ALU.mult, ALU.add), p0)
            d3 = dve.then(lambda: V.tensor_tensor_scan(B["EKV"][:, ::-1], dc, B["EKV"][:, ::-1], 0.0, ALU.mult, ALU.add))
            q0 = pool.put(lambda: G.tensor_tensor(B["NF"][:, :], B["NF"][:, :], B["EKV"][:, :], ALU.add), d3)
            q1 = pool.put(lambda: G.tensor_tensor(B["NF"][:, :], B["NF"][:, :], k[:, :], ALU.add), q0, p2)
            wk["kfree"][s] = q1
            yield
            t3 = dve.put(lambda: V.tensor_scalar(B["DF"][:, :], B["DF"][:, :], 1e-8, None, ALU.max), t2)
            t4 = dve.put(lambda: V.reciprocal(B["DF"][:, :], B["DF"][:, :]), t3)
            yield
            t5 = dve.put(lambda: V.scalar_tensor_tensor(out=B["NF"][:, :], in0=B["NF"][:, :], scalar=cs[:, 5, b:b + 1],
                                                        in1=B["DF"][:, :], op0=ALU.mult, op1=ALU.mult), t4, q1, t_cs)
            yield
            h = b % 2
            while (l, b) not in rt_free:
                yield
            yield from bank.take()

            def tr():
                for q in range(4):
                    m = nc.tensor.transpose(bank.t[:, q * P:q * P + P], B["NF"][:, q * P:q * P + P], ident)
                return m
            m = pe.put(tr, t5, t_c, bank.tok)
            wk["free"][s] = m
            e = act.put(lambda: A.copy(RT[h][:, :, c * P:c * P + P], bank.t[:, :].rearrange("p (q c) -> p q c", q=4)),
                        m, *rt_free[l, b])
            bank.give(e)
            wk["done"] += 1
            if c == 3:
                rt_ready[l, b] = e

        xs = dict(n=0, free=[None] * len(XSp))
        xt = dict(n=0, free=[None] * len(XT))
        fr = dict(xr=[(), ()], ht=None, lg={}, done=0, base=None)
        tile_xs, tile_x, lgt, xrow = {}, {}, {}, {}

        def load_x(l, i, *after):
            s = xt["n"] % len(XT)
            xt["n"] += 1
            src = (xtok if l == 0 else Y0)[i * P:i * P + P, :]
            tile_x[l, i] = (s, r_x.start(sp, s, lambda: S.dma_start(XT[s][:, :], src), xt["free"][s], *after))

        def front(l, i, bx, bl):
            s, t_x = tile_x[l, i]
            o = i % 2
            b, q = divmod(i, 4)
            R = XR[o]
            rt = RT[b % 2][:, q, :]
            E = LAYERS[l]["E"]
            a = act.put(lambda: A.activation(R[:, :], XT[s][:, :], ACT.Tanh, scale=0.5), t_x, *fr["xr"][o])
            yield
            a = dve.put(lambda: V.scalar_tensor_tensor(out=R[:, :], in0=R[:, :], scalar=1.0, in1=rt,
                                                       op0=ALU.add, op1=ALU.mult), a, rt_ready[l, b])
            fr["base"] = a
            fr["nbase", l] = i + 1
            if q == 3:
                nxt = (l, b + 2) if b < 2 else (1, b - 2)
                if l == 0 or b < 2:
                    rt_free[nxt] = [a]
            if l == 0:
                yield
                c = act.then(lambda: A.activation(BS[:, :], R[:, :], ACT.Square, accum_out=sm[:, i, 0:1]), a)
                yield
                c = dve.put(lambda: V.tensor_scalar(sm[:, i, 1:2], sm[:, i, 0:1], 1.0 / D, 1e-6, ALU.mult, ALU.add), c)
                c = pool.put(lambda: G.tensor_tensor(sm[:, i, 2:3], sm[:, i, 1:2], half[:, :], ALU.pow), c, t_half)
                yield
                a = dve.put(lambda: V.scalar_tensor_tensor(out=R[:, :], in0=R[:, :], scalar=sm[:, i, 2:3],
                                                           in1=rmsb[:, :], op0=ALU.mult, op1=ALU.mult), c, t_c)
            w = r_xr[l].start(sp, o, lambda: S.dma_start(X[l][i * P:i * P + P, 0:D], R[:, :]), a)
            xrow[l, i] = w
            yield
            yield from bx.take()

            def tr():
                for q in range(4):
                    m = nc.tensor.transpose(bx.t[:, q * P:q * P + P], R[:, q * P:q * P + P], ident)
                return m
            m = pe.put(tr, a, bx.tok, t_c)
            fr["xr"][o] = (w, m)
            z = xs["n"] % len(XSp)
            xs["n"] += 1
            c = act.put(lambda: A.copy(HT32[:, :], bx.t[:, :]), m, fr["ht"])
            h = act.put(lambda: A.activation(XSp[z][:, 0, :], bx.t[:, :], ACT.Copy, scale=XS), m, xs["free"][z])
            yield
            lo = dve.put(lambda: V.scalar_tensor_tensor(out=XSp[z][:, 1, :], in0=bx.t[:, :], scalar=XS,
                                                        in1=XSp[z][:, 0, :], op0=ALU.mult, op1=ALU.subtract), h)
            tile_xs[l, i] = (z, lo)
            bx.give(lo)
            yield from bl.take()

            def lgm():
                for q in range(4):
                    m = nc.tensor.matmul(bl.t[:, 0:E], HT32[:, q * P:q * P + P], rw[l][:, q, :],
                                         start=(q == 0), stop=(q == 3))
                return m
            m = pe.put(lgm, c, bl.tok, t_c)
            fr["ht"] = m
            while q == 0 and b and (l, b - 1) not in fr["lg"]:
                yield
            t = dve.put(lambda: V.tensor_copy(lg[:, q, 0:E], bl.t[:, 0:E]), m, fr["lg"].get((l, b - 1)))
            bl.give(t)
            lgt[l, i] = t

        rb = dict(mask=None, mac=None)
        wd_tok = {0: [None, None], 1: [None, None]}

        def bc(ap, shape):
            return ap.to_broadcast(shape)

        def route(l, b, bl):
            L = LAYERS[l]
            E, K = L["E"], L["K"]
            for q in range(4):
                t = lgt[l, 4 * b + q]
                a = dve.then(lambda q=q: V.max(mx[:, q, :], lg[:, q, 0:E]), t)
                dve.then(lambda q=q: V.max_index(ix[:, q, :], mx[:, q, :], lg[:, q, 0:E]), a)
            yield
            psl = bl.t
            m0 = mx[:, :, 0:1]
            o = (OH[:, b * 64:b * 64 + 64] if l == 0 else OH[:, 0:4 * K * E]).rearrange("p (q k e) -> p q k e", q=4, k=K)
            ot = OT[:, 0:4 * K * E].rearrange("p (q k e) -> p q k e", q=4, k=K)
            a = dve.then(lambda: V.tensor_tensor(ex[:, :, 0:E], lg[:, :, 0:E], bc(m0, [P, 4, E]), ALU.subtract))
            c = dve.then(lambda: V.tensor_tensor(et[:, :, 0:K], mx[:, :, 0:K], bc(m0, [P, 4, K]), ALU.subtract))
            fr["lg"][l, b] = a
            a = act.put(lambda: A.activation(ex[:, :, 0:E], ex[:, :, 0:E], ACT.Exp), a)
            c = act.put(lambda: A.activation(et[:, :, 0:K], et[:, :, 0:K], ACT.Exp), c)
            x = dve.then(lambda: V.tensor_copy(ixf[:, :, 0:K], ix[:, :, 0:K]))
            x = dve.then(lambda: V.tensor_tensor(
                o, bc(iota[:, 0:E].unsqueeze(1).unsqueeze(1), [P, 4, K, E]),
                bc(ixf[:, :, 0:K].unsqueeze(3), [P, 4, K, E]), ALU.is_equal), x)
            yield
            mk = dve.then(lambda: V.tensor_reduce(mask[:, :, 0:E], o.rearrange("p q k e -> p q e k"), AX_X, ALU.add),
                         x, rb["mask"])
            a = dve.then(lambda: V.tensor_reduce(s1[:, :, :], ex[:, :, 0:E], AX_X, ALU.add), a)
            a = dve.then(lambda: V.reciprocal(s1[:, :, :], s1[:, :, :]), a)
            yield
            if l == 1:
                a = dve.then(lambda: V.tensor_scalar(s1[:, :, :], s1[:, :, :], UN, None, ALU.mult), a)
            a = dve.then(lambda: V.tensor_tensor(et[:, :, 0:K], et[:, :, 0:K], bc(s1[:, :, :], [P, 4, K]), ALU.mult), a, c)
            if l == 0:
                a = dve.then(lambda: V.tensor_reduce(s2[:, :, :], et[:, :, 0:K], AX_X, ALU.add), a)
                a = dve.then(lambda: V.reciprocal(s2[:, :, :], s2[:, :, :]), a)
                a = dve.then(lambda: V.tensor_scalar(s2[:, :, :], s2[:, :, :], UN, None, ALU.mult), a)
                a = dve.then(lambda: V.tensor_tensor(et[:, :, 0:K], et[:, :, 0:K], bc(s2[:, :, :], [P, 4, K]), ALU.mult), a)
            a = dve.then(lambda: V.tensor_tensor(ot, o, bc(et[:, :, 0:K].unsqueeze(3), [P, 4, K, E]), ALU.mult), a)
            a = dve.then(lambda: V.tensor_reduce(Wd[b % 2][:, :, 0:E], ot.rearrange("p q k e -> p q e k"), AX_X, ALU.add),
                        a, wd_tok[l][b % 2], wd_tok[0][b % 2])
            wd_tok[l][b % 2] = r_wd[l].start(sp, b % 2, lambda: S.dma_start(
                X[l][b * 512:b * 512 + 512, D:D + E].rearrange("(q p) e -> p q e", p=P), Wd[b % 2][:, :, 0:E]), a)
            yield
            n = dve.then(lambda: V.tensor_reduce(mred[:, 0:E], mask[:, :, 0:E].rearrange("p q e -> p e q"), AX_X, ALU.add), mk)
            if b == 0:
                n = dve.then(lambda: V.tensor_copy(macc[1][:, 0:E], mred[:, 0:E]), n, rb["mac"])
            else:
                n = dve.then(lambda: V.tensor_tensor(macc[b + 1][:, 0:E], macc[b][:, 0:E], mred[:, 0:E], ALU.add), n)

            def excl():
                for q in range(4):
                    outp = psl[:, q * E:q * E + E]
                    m = nc.tensor.matmul(outp, U16[:, :], mask[:, q, 0:E], start=True, stop=(q == 0 and b == 0))
                    for r in range(q):
                        m = nc.tensor.matmul(outp, ones16[:, :], mask[:, r, 0:E], start=False,
                                             stop=(r == q - 1 and b == 0))
                    if b:
                        m = nc.tensor.matmul(outp, ones16[:, :], macc[b][:, 0:E], start=False, stop=True)
                return m
            yield from bl.take()
            m = pe.put(excl, mk, n, t_c16, bl.tok)
            rb["mask"] = m
            rb["mac"] = m
            if l == 0:
                pb = posb[:, b * 32:b * 32 + 32]
                yield
                t = dve.then(lambda: V.tensor_copy(pb, psl[:, 0:32]), m)
                bl.give(t)
                rb["n", l] = b + 1
                return
            yield
            t = dve.then(lambda: V.tensor_tensor(
                ot, o, bc(psl[:, 0:4 * E].rearrange("p (q e) -> p q e", q=4).unsqueeze(2), [P, 4, K, E]), ALU.mult), m, a)
            bl.give(t)
            ks = slice(b * 4 * K, (b + 1) * 4 * K)
            t = dve.then(lambda: V.tensor_reduce(gq[:, ks].rearrange("p (q k) -> p q k", q=4), ot, AX_X, ALU.add), t)
            t = split_slot(ks, t)
            yield
            t = dve.then(lambda: V.scalar_tensor_tensor(out=ja[:, ks].rearrange("p (q k) -> p q k", q=4),
                                                       in0=ixf[:, :, 0:K], scalar=4.0,
                                                       in1=gj[:, ks].rearrange("p (q k) -> p q k", q=4),
                                                       op0=ALU.mult, op1=ALU.add), t)
            t = dve.then(lambda: V.tensor_scalar(gj[:, ks], gq[:, ks], float(CAP), -1000.0, ALU.is_ge, ALU.mult), t)
            rb["slots"] = dve.then(lambda: V.tensor_tensor(qa[:, ks], qa[:, ks], gj[:, ks], ALU.add), t)
            rb["n", l] = b + 1

        def split_slot(ks, t):
            t = dve.then(lambda: V.tensor_copy(gi[:, ks], gq[:, ks]), t)
            t = dve.then(lambda: V.tensor_single_scalar(gi[:, ks], gi[:, ks], 7, ALU.arith_shift_right), t)
            t = dve.then(lambda: V.tensor_copy(gj[:, ks], gi[:, ks]), t)
            return dve.then(lambda: V.scalar_tensor_tensor(out=qa[:, ks], in0=gj[:, ks], scalar=-128.0, in1=gq[:, ks],
                                                          op0=ALU.mult, op1=ALU.add), t)

        def starts0(bl):
            yield from bl.take()
            psl = bl.t
            m = pe.put(lambda: nc.tensor.matmul(psl[:, 0:8], ones16[:, :], macc[4][:, 0:8], start=True, stop=True),
                       bl.tok, rb["mac"], (dve.sem, dve.n))
            rb["mac"] = m
            t = dve.then(lambda: V.tensor_scalar(cni[:, :], psl[:, 0:8], 127.0, None, ALU.add), m)
            bl.give(t)
            yield
            t = dve.then(lambda: V.tensor_single_scalar(cni[:, :], cni[:, :], 7, ALU.arith_shift_right), t)
            t = dve.then(lambda: V.tensor_copy(cn[:, 0, :], cni[:, :]), t)
            t = dve.then(lambda: V.tensor_tensor_scan(cn[:, 1, :], ones[:, :], cn[:, 0, :], 0.0, ALU.mult, ALU.add), t)
            t = dve.then(lambda: V.tensor_tensor(cn[:, 2, :], cn[:, 1, :], cn[:, 0, :], ALU.subtract), t)
            t = dve.then(lambda: V.tensor_scalar(cn[:, 2, :], cn[:, 2, :], 128.0, None, ALU.mult), t)
            pv = posb[:, :].rearrange("p (i e) -> p i e", i=16)
            ov = OH[:, 0:256].rearrange("p (i k e) -> p i k e", i=16, k=2)
            t = dve.then(lambda: V.tensor_tensor(pv, pv, bc(cn[:, 2:3, :], [P, 16, 8]), ALU.add), t)
            t = dve.then(lambda: V.tensor_tensor(ov, ov, bc(pv.unsqueeze(2), [P, 16, 2, 8]), ALU.mult), t)
            ks = slice(0, 32)
            t = dve.then(lambda: V.tensor_reduce(gq[:, ks].rearrange("p (i k) -> p i k", i=16), ov, AX_X, ALU.add), t)
            t = split_slot(ks, t)
            rb["slots"] = dve.then(lambda: V.tensor_copy(ja[:, ks], gj[:, ks]), t)
            yield
            u = dve.then(lambda: V.tensor_tensor(ohB[:, :, :], bc(cn[:, 1:2, :], [P, 39, 8]),
                                                bc(iota[:, 0:39].unsqueeze(2), [P, 39, 8]), ALU.is_le))
            u = dve.then(lambda: V.tensor_reduce(ebf[:, :].unsqueeze(2), ohB[:, :, :], AX_X, ALU.add), u)
            u = dve.then(lambda: V.tensor_scalar(ebf[:, :], ebf[:, :], 7.0, None, ALU.min), u)
            dve.then(lambda: V.tensor_copy(ebi, ebf[:, :]), u)
            u = dve.then(lambda: V.tensor_tensor(ohB[:, :, :], bc(iota[:, 0:8].unsqueeze(1), [P, 39, 8]),
                                                bc(ebf[:, :].unsqueeze(2), [P, 39, 8]), ALU.is_equal), u)
            rb["experts"] = u
            yield from tables(0, bl)

        def tables(l, bl):
            L = LAYERS[l]
            K, NB = L["K"], L["NB"]
            t = rb["slots"]
            free = [None, None]
            yield from bl.take()
            psl = bl.t
            for g in range(4 * K):
                s = g % 2
                for r in range(4):
                    n = 4 * g + r
                    i = n // K
                    dve.put(lambda s=s, r=r, n=n: V.tensor_scalar(A16[s][:, r, :], iota16[:, :], qa[:, n:n + 1], None,
                                                                  ALU.is_equal), t, free[s], *rb["ab"])
                    d = dve.put(lambda s=s, r=r, n=n, i=i: V.tensor_scalar(
                        B16[s][:, r, 0:NB], iota16[:, 0:NB], ja[:, n:n + 1], tid[:, i:i + 1], ALU.is_equal, ALU.mult))

                def mm(g=g, s=s):
                    for r in range(4):
                        m = nc.tensor.matmul(psl[:, 0:NB], A16[s][:, r, :], B16[s][:, r, 0:NB],
                                             start=(g == 0 and r == 0), stop=(g == 4 * K - 1 and r == 3))
                    return m
                free[s] = pe.put(mm, d, bl.tok)
                yield
            m = free[(4 * K - 1) % 2]
            rb["tab"] = m
            t = dve.put(lambda: V.scalar_tensor_tensor(out=idf[:, 0:NB], in0=psl[:, 0:NB], scalar=0.0,
                                                       in1=dconst[:, 0:NB], op0=ALU.is_equal, op1=ALU.mult), m)
            t = dve.put(lambda: V.scalar_tensor_tensor(out=idx[l][:, 0:NB], in0=psl[:, 0:NB], scalar=-1.0,
                                                       in1=idf[:, 0:NB], op0=ALU.add, op1=ALU.add), t)
            bl.give(t)
            rb["table", l] = t

        wt = dict(n=0, free=[None] * 2)

        def wload(src, dst, pieces, *after, low="pool"):
            out = []
            for c0, cw in pieces:
                s = wt["n"] % 2
                wt["n"] += 1
                t = r_st.start(sp, s, lambda s=s, c0=c0, cw=cw: S.dma_start(ST[s][:, 0:cw], src[:, c0:c0 + cw]),
                               wt["free"][s])
                hi = Whi[:, dst + c0:dst + c0 + cw]
                lo = Wlo[:, dst + c0:dst + c0 + cw]
                if low == "pool":
                    a = act.put(lambda s=s, cw=cw: A.activation(ST[s][:, 0:cw], ST[s][:, 0:cw], ACT.Copy, scale=WS), t)
                    a = act.put(lambda s=s, cw=cw, hi=hi: A.copy(hi, ST[s][:, 0:cw]), a, *after)
                    a = pool.put(lambda s=s, cw=cw, hi=hi, lo=lo: G.tensor_tensor(lo, ST[s][:, 0:cw], hi, ALU.subtract),
                                 a, *after)
                else:
                    a = act.put(lambda s=s, cw=cw, hi=hi: A.activation(hi, ST[s][:, 0:cw], ACT.Copy, scale=WS), t, *after)
                    a = dve.put(lambda s=s, cw=cw, hi=hi, lo=lo: V.scalar_tensor_tensor(
                        out=lo, in0=ST[s][:, 0:cw], scalar=WS, in1=hi, op0=ALU.mult, op1=ALU.subtract), a, *after)
                wt["free"][s] = a
                out.append(a)
            return out

        blocks = []
        st = dict(g=0, h=[None, None], hs=[None, None], o=[None, None], ob=[None] * 4, sg=None,
                  gf=[None, None], chain=[], last=None, xg=[None] * 3, px=None, ph=None, lo=0, ended=0)

        def gather(n):
            if n >= len(blocks) or blocks[n]["kind"] != "routed" or "g" in blocks[n]:
                return
            B = blocks[n]
            l, j = B["l"], B["j"]
            s = st["g"] % 3
            st["g"] += 1
            w = D + LAYERS[l]["E"]
            B["xg"] = s
            B["g"] = r_g.start(pool, s, lambda: G.indirect_dma_start(
                out=XG[s][:, 0:w], out_offset=None, in_=X[l][:, :],
                in_offset=bass.IndirectOffsetOnAxis(ap=idx[l][:, j:j + 1], axis=0)), B["ready"], t_dummy, *B["rows"],
                *(st["xg"][s] or ()))

        def turn(n):
            if n >= len(blocks) or blocks[n]["kind"] != "routed":
                return
            B = blocks[n]
            l, s, j = B["l"], B["xg"], B["j"]
            w = WSL[:, n % 8:n % 8 + 1]

            def tr():
                for q in range(4):
                    m = nc.tensor.transpose(psX[:, q * P:q * P + P], XG[s][:, q * P:q * P + P], ident)
                return m
            m = pe.put(tr, B["g"], st["px"])
            if l == 0:
                u = dve.put(lambda: V.tensor_tensor_reduce(jnk[:, :], XG[s][:, D:D + 8], ohB[:, j, :], 1.0, 0.0,
                                                           ALU.mult, ALU.add, w), B["g"], st.get("u"))
            else:
                e = j // 4
                u = dve.put(lambda: V.tensor_copy(w, XG[s][:, D + e:D + e + 1]), B["g"])
            st["u"] = u
            B["u"] = u
            st["xg"][s] = (m, u)
            z = xs["n"] % len(XSp)
            xs["n"] += 1
            h = act.put(lambda: A.activation(XSp[z][:, 0, :], psX[:, :], ACT.Copy, scale=XS), m, xs["free"][z])
            lo = dve.put(lambda: V.scalar_tensor_tensor(out=XSp[z][:, 1, :], in0=psX[:, :], scalar=XS,
                                                        in1=XSp[z][:, 0, :], op0=ALU.mult, op1=ALU.subtract), h)
            st["px"] = lo
            B["xs"] = (z, lo)

        def gu(n):
            B = blocks[n]
            l = B["l"]
            F = LAYERS[l]["F"]
            z, t = B["xs"]
            a = n % 2
            hx = XSp[z]

            def mm():
                if B.get("reg"):
                    j = B["j"]
                    r = nc.tensor.value_load(ebi[0:1, j:j + 1], min_val=0, max_val=7)
                    B["rv"] = r

                    def w(half, off, n):
                        return half[:, bass.ds(r * 3072 + off, n)]
                else:
                    def w(half, off, n):
                        return half[:, B["w"] + off:B["w"] + off + n]
                B["wf"] = w
                if l == 0:
                    outs = [(psG[a][0][:, 0:512], 0, 512)]
                else:
                    outs = [(psG[a][0][:, 0:F], 0, F), (psG[a][1][:, 0:F], F, F)]
                for q in range(4):
                    off = q * 2 * F
                    for x, half in ((0, Whi), (0, Wlo), (1, Whi)):
                        first, last = q == 0 and x == 0 and half is Whi, q == 3 and x == 1
                        for o, c, nn in outs:
                            m = nc.tensor.matmul(o, hx[:, x, q * P:q * P + P], w(half, off + c, nn),
                                                 start=first, stop=last)
                return m
            m = pe.put(mm, t, st["gf"][a], *B["wt"])
            B["gu"] = m
            if B.get("endx", True):
                xs["free"][z] = m
            post.append(lambda: gu_ew(n, m))

        def gu_ew(n, m):
            B = blocks[n]
            l, a = B["l"], n % 2
            F = LAYERS[l]["F"]
            g, u = (psG[a][0][:, 0:F], psG[a][0][:, F:2 * F]) if l == 0 else (psG[a][0][:, 0:F], psG[a][1][:, 0:F])
            H = H32[a][:, 0:F]
            s = act.put(lambda: A.activation(H, g, ACT.Tanh, scale=0.5 * UN), m, st["h"][a])
            s = dve.put(lambda: V.scalar_tensor_tensor(out=H, in0=H, scalar=1.0, in1=g, op0=ALU.add, op1=ALU.mult), s)
            h = dve.put(lambda: V.scalar_tensor_tensor(out=H, in0=H, scalar=0.5 * XS * UN * UN, in1=u,
                                                       op0=ALU.mult, op1=ALU.mult), s)
            st["gf"][a] = h
            B["h"] = h

        def hturn(n):
            B = blocks[n]
            a = n % 2
            NK = LAYERS[B["l"]]["NK"]

            def tr():
                for q in range(NK):
                    m = nc.tensor.transpose(psH[:, q * P:q * P + P], H32[a][:, q * P:q * P + P], ident)
                return m
            m = pe.put(tr, B["h"], st["ph"])
            st["h"][a] = m
            post.append(lambda: hturn_ew(n, m))

        def hturn_ew(n, m):
            B = blocks[n]
            a = n % 2
            w = LAYERS[B["l"]]["NK"] * P
            h = act.put(lambda: A.copy(HS[a][:, 0, 0:w], psH[:, 0:w]), m, st["hs"][a])
            lo = dve.put(lambda: V.tensor_tensor(HS[a][:, 1, 0:w], psH[:, 0:w], HS[a][:, 0, 0:w], ALU.subtract), h)
            st["ph"] = lo
            B["hs"] = lo

        def down(n):
            B = blocks[n]
            l, a = B["l"], n % 2
            L = LAYERS[l]
            NK = L["NK"]
            o = B.get("bank", B["o"] % 2)
            off0 = 8 * L["F"]

            def mm():
                for q in range(NK):
                    for x, half in ((0, Whi), (0, Wlo), (1, Whi)):
                        m = nc.tensor.matmul(psO[o][:, :], HS[a][:, x, q * P:q * P + P],
                                             B["wf"](half, off0 + q * 512, 512),
                                             start=(q == 0 and x == 0 and half is Whi and B["first"]),
                                             stop=(q == NK - 1 and x == 1 and B["last"]))
                return m
            m = pe.put(mm, B["hs"], st["o"][o] if B["first"] else None)
            st["hs"][a] = m
            B["done"] = m
            st["done"] = m
            if B["last"]:
                post.append(lambda: down_ew(n, m))

        def down_ew(n, m):
            B = blocks[n]
            l = B["l"]
            o = B.get("bank", B["o"] % 2)
            k = B["o"] % 4
            if B["kind"] == "shared":
                s, _ = tile_x[l, B["i"]]
                i = B["i"]
                t = dve.put(lambda: V.scalar_tensor_tensor(out=OB[k][:, :], in0=psO[o][:, :], scalar=UN,
                                                           in1=XT[s][:, :], op0=ALU.mult, op1=ALU.add), m, st["ob"][k])
                xt["free"][s] = t
                w = r_y.start(sp, k, lambda: S.dma_start(Y[l][i * P:i * P + P, :], OB[k][:, :]), t)
                st["chain"].append(w)
                st["ended"] = i + 1
            else:
                j = B["j"]
                t = act.put(lambda: A.activation(OB[k][:, :], psO[o][:, :], ACT.Copy,
                                                 scale=WSL[:, n % 8:n % 8 + 1]), m, B["u"], st["ob"][k])
                if l == 0 or j % 4 == 0:
                    st["cur"] = st["chain"]
                    st["chain"] = []
                w = r_o.start(pool, k, lambda: G.indirect_dma_start(
                    out=Y[l][:, :], out_offset=bass.IndirectOffsetOnAxis(ap=idx[l][:, j:j + 1], axis=0),
                    in_=OB[k][:, :], in_offset=None, compute_op=ALU.add), t, t_dummy, *st["cur"])
                st["chain"].append(w)
            st["o"][o] = t
            st["ob"][k] = w

        post = []

        def drain():
            while post:
                post.pop(0)()

        def step(n):
            gather(n + 3)
            turn(n + 1)
            gu(n)
            tasks.turn()
            drain()
            rest(n)
            drain()

        def rest(n):
            if n - 1 >= st["lo"]:
                hturn(n - 1)
            if n - 2 >= st["lo"]:
                down(n - 2)

        def flush():
            n = len(blocks)
            drain()
            hturn(n - 1)
            down(n - 2)
            drain()
            down(n - 1)
            drain()
            st["lo"] = n

        no = [0]

        def add(**kw):
            kw.setdefault("first", True)
            kw.setdefault("last", True)
            kw["o"] = no[0]
            if kw["last"]:
                no[0] += 1
            blocks.append(kw)
            return len(blocks) - 1

        tasks = Tasks()
        bX, bF, bL, bO = Bank(psX), Bank(psG[0][1]), Bank(psG[1][1]), Bank(psO[1])
        rb["ab"] = []

        def fronts(l, wkvs, bw, bx, bl, done, xready, shared, weights, after_fronts, turns):
            st["ended"] = 0
            xt["base"] = xt["n"]
            nf = ns = nr = nx = 0
            live = []
            routing = [None]
            rb["n", l] = 0
            fr["nbase", l] = 0
            tailed = False

            def counted(gen, what):
                yield from gen
                what[0] += 1
            fin = [0]
            wfin = [0]
            wst = 0
            while ns < NT or not tailed or tasks.live:
                if wkvs and wst - wfin[0] < 2:
                    tasks.start(counted(wkv(*wkvs.pop(0), bw), wfin))
                    wst += 1
                while nx < NT and nx < st["ended"] + 4 and nx <= nf + 2:
                    load_x(l, nx, *xready)
                    nx += 1
                if nf < nx and nf - fin[0] < 2 and (l, nf // 4) in rt_ready:
                    tasks.start(counted(front(l, nf, bx, bl), fin))
                    nf += 1
                if nr < 4 and fin[0] >= 4 * nr + 4 and rb["n", l] == nr:
                    tasks.start(route(l, nr, bl))
                    nr += 1
                if not tailed and rb["n", l] == 4:
                    tasks.start(after_fronts())
                    tailed = True
                tasks.turn()
                drain()
                weights()
                lag = 0 if fin[0] == NT else turns["lag"]
                if ns < NT and ns + lag < fin[0]:
                    for sub in range(shared(ns)):
                        for _ in range(turns["sub"] if not tailed else turns["tail"]):
                            tasks.turn()
                    ns += 1

        def tables1():
            rb["ab"] = [fr["base"]]
            yield from tables(1, bO)

        wsh, w0 = [], []
        wl = [lambda c=c: wsh.extend(wload(W0[8], 7 * 3072, [c])) for c in WCH[0]]
        wl += [lambda e=e, c=c: w0.extend(wload(W0[e], e * 3072, [c])) for e in range(7) for c in WCH[0]]
        cnt = [0]

        def weights0():
            cnt[0] += 1
            if wl and cnt[0] % 2 == 0:
                wl.pop(0)()

        def shared0(i):
            n = add(kind="shared", l=0, i=i, xs=tile_xs[0, i], w=7 * 3072, wt=[wsh[-1]])
            gu(n)
            rest(n)
            return 1

        def tail0():
            RTlast = [fr["base"]]
            rb["ab"] = RTlast
            yield from starts0(bL)

        fronts(0, [(0, b, c) for b in range(4) for c in range(4)], bX, bF, bL, None, [], shared0, weights0, tail0,
               dict(lag=0, sub=0, tail=2))
        flush()
        while wl:
            wl.pop(0)()
        w0 += wload(W0[7], 7 * 3072, WCH[0], st["done"])
        rt_free[1, 1] = [fr["base"], rb["tab"]]
        base = len(blocks)
        rows = [xrow[0, 14], xrow[0, 15]] + wd_tok[0]
        for j in range(39):
            add(kind="routed", l=0, j=j, reg=True, ready=rb["table", 0], rows=rows, wt=[w0[-1], rb["experts"]])
        for n in (base, base + 1, base + 2):
            gather(n)
        st["px"] = bX.tok
        turn(base)
        todo = [(1, b, c) for b in range(2) for c in range(4)]
        wfin, wst = wk["done"], wk["n"]
        for n in range(base, base + 39):
            if todo and wk["n"] - wk["done"] < 2:
                tasks.start(wkv(*todo.pop(0), bF))
            step(n)
        while tasks.live or todo:
            if todo and wk["n"] - wk["done"] < 2:
                tasks.start(wkv(*todo.pop(0), bF))
            tasks.turn()
        flush()
        end0 = st["done"]
        done0 = list(st["chain"])

        st["chain"] = []
        order = [32, 33] + list(range(32))
        slot = {e: (m % 5) * 4352 for m, e in enumerate(order)}
        wtok, last_use = {}, {}

        def load1(m, piece, low="dve"):
            e = order[m]
            after = end0 if m < 5 else last_use[order[m - 5]]
            wtok[e] = wload(W1[e], slot[e], [WCH[1][piece]], after, low=low)[-1]

        wl = [(m, c) for m in range(2, 5) for c in range(4)]
        for m in range(2):
            for c in range(4):
                load1(m, c)
        bX.tok = st["px"]
        bO.tok = st["o"][1]
        cnt = [0]

        def weights1():
            pass

        def shared1(i):
            for hf in range(2):
                n = add(kind="shared", l=1, i=i, xs=tile_xs[1, i], w=slot[32 + hf], wt=[wtok[32 + hf]], bank=0,
                        first=(hf == 0), last=(hf == 1), endx=(hf == 1))
                gu(n)
                tasks.turn()
                drain()
                rest(n)
                tasks.turn()
                drain()
            if wl and i >= 1:
                load1(*wl.pop(0))
            return 0


        fronts(1, [(1, b, c) for b in (2, 3) for c in range(4)], bX, bX, bO, None, done0, shared1, weights1,
               lambda: tables1(), dict(lag=0, sub=0, tail=0))
        while wl:
            load1(*wl.pop(0))
        st["o"][1] = bO.tok
        st["px"] = bX.tok
        base = len(blocks)
        rows = [xrow[1, 14], xrow[1, 15]] + wd_tok[1]
        for j in range(128):
            add(kind="routed", l=1, j=j, ready=rb["table", 1], rows=rows, w=slot[j // 4])
        for n in (base, base + 1, base + 2):
            gather(n)
        turn(base)
        for g in range(128):
            n = base + g
            blocks[n]["wt"] = [wtok[g // 4]]
            step(n)
            if g == 2:
                last_use[32] = last_use[33] = blocks[base - 1]["done"]
            if g % 4 == 2 and g > 4:
                last_use[g // 4 - 1] = blocks[base + g - 3]["done"]
            if 3 <= g < 7:
                for c in (2 * (g - 3), 2 * (g - 3) + 1):
                    load1(5 + c // 4, c % 4)
            elif g >= 7 and 7 + (g - 7) // 4 < 34:
                load1(7 + (g - 7) // 4, (g - 7) % 4)
        flush()
        last = [(r_o.sems[k], r_o.v[k]) for k in range(4)] + [(r_y.sems[k], r_y.v[k]) for k in range(4)]
        sp.wait(last)

        block = ctx.enter_context(nc.Block())

        @block.sync
        def _(eng):
            sp.run(eng)

        @block.gpsimd
        def _(eng):
            pool.run(eng)

        @block.scalar
        def _(eng):
            act.run(eng)

        @block.vector
        def _(eng):
            dve.run(eng)

        @block.tensor
        def _(eng):
            pe.run(eng)


def kernel(**inputs):
    import numpy as np
    import concourse.bacc as bacc
    from concourse.bass_utils import run_bass_kernel_spmd

    f = {k: np.asarray(v) for k, v in inputs.items()}
    x = np.ascontiguousarray(f["x"].reshape(2048, 512))
    fT = np.ascontiguousarray(f["fside_BxSxS_0"].reshape(2048, 512).T)
    cst = np.zeros((128, 528), np.float32)
    p = np.arange(128)
    cst[:, 0:128] = np.eye(128)
    cst[:, 128:256] = p[None, :]
    cst[:, 256:384] = p[:, None] < p[None, :]
    cst[:, 384:512] = 2049 + 128 * (p[None, :] % 4) + p[:, None]
    cst[:, 512:528] = 128 * np.arange(16)[None, :] + p[:, None] + 1

    def cols(v):
        return v.reshape(4, 128).T

    svec = np.ascontiguousarray(np.concatenate(
        [cols(f[n]) for n in ("L0_cond_w", "L1_cond_w", "L0_cond_u", "L1_cond_u")], axis=1))
    cond = np.ascontiguousarray(np.broadcast_to(f["cond_512"][None], (128, 4, 128)))
    rms = np.ascontiguousarray(np.broadcast_to(f["L0_ffn_rms_weight"][None], (128, 512)))
    rout = np.ascontiguousarray(f["L0_ffn_router_w"].reshape(4, 128, 8).transpose(1, 0, 2))
    gatew = np.ascontiguousarray(f["L1_ffn_gate_w"].T.reshape(4, 128, 32).transpose(1, 0, 2))

    def pack(gate, up, downw, nk):
        e, _, F = gate.shape
        gu = np.concatenate([gate, up], axis=2).reshape(e, 4, 128, 2 * F).transpose(0, 2, 1, 3).reshape(e, 128, 8 * F)
        dp = np.zeros((e, nk * 128, 512), np.float32)
        dp[:, :F] = downw
        dp = dp.reshape(e, nk, 128, 512).transpose(0, 2, 1, 3).reshape(e, 128, nk * 512)
        return np.ascontiguousarray(np.concatenate([gu, dp], axis=2))

    W0 = pack(np.concatenate([f["L0_ffn_w_gate"], f["L0_ffn_sw_gate"][None]]),
              np.concatenate([f["L0_ffn_w_up"], f["L0_ffn_sw_up"][None]]),
              np.concatenate([f["L0_ffn_w_down"], f["L0_ffn_sw_down"][None]]), 2)

    def halves(a):
        return a.reshape(512, 2, 352).transpose(1, 0, 2)

    W1 = pack(np.concatenate([f["L1_ffn_w1"], halves(f["L1_ffn_sw1"])]),
              np.concatenate([f["L1_ffn_w3"], halves(f["L1_ffn_sw3"])]),
              np.concatenate([f["L1_ffn_w2"], f["L1_ffn_sw2"].reshape(2, 352, 512)]), 3)

    nc = bacc.Bacc("TRN2", target_bir_lowering=False, num_devices=1)
    arrays, args = {}, []
    for name, a in (("x", x), ("fT", fT), ("cst", cst), ("svec", svec), ("cond", cond), ("rms", rms),
                    ("rout", rout), ("gatew", gatew), ("W0", W0), ("W1", W1)):
        arrays[name] = a
        args.append(nc.dram_tensor(name, list(a.shape), mybir.dt.from_np(a.dtype), kind="ExternalInput").ap())
    out = nc.dram_tensor("out", [ROWS, D], F32, kind="ExternalOutput").ap()
    build(nc, *args, out)
    r = run_bass_kernel_spmd(nc, [arrays], core_ids=[0])
    return r.results[0]["out"][:2048].reshape(4, 512, 512)
```

```python
from contextlib import ExitStack

import concourse.bass as bass
from concourse import mybir

P = 128
T = 2048
D = 512
NT = T // P
ROWS = T + 512
CAP = 512
F32 = mybir.dt.float32
F16 = mybir.dt.float16
I32 = mybir.dt.int32
U32 = mybir.dt.uint32
ALU = mybir.AluOpType
ACT = mybir.ActivationFunctionType
AX_X = mybir.AxisListType.X

XS = 8.0
WS = 64.0
UN = 1.0 / (XS * WS)

LAYERS = (
    dict(E=8, K=2, F=256, NK=2, NB=39, W=3072),
    dict(E=32, K=6, F=352, NK=3, NB=128, W=4352),
)
WCH = (((0, 1024), (1024, 1024), (2048, 1024)), ((0, 1088), (1088, 1088), (2176, 1088), (3264, 1088)))


class Line:

    def __init__(self, sem):
        self.sem, self.n, self.todo, self.seen = sem, 0, [], {}

    def wait(self, after):
        for tok in after:
            if tok is None:
                continue
            sem, v = tok
            if self.seen.get(id(sem), 0) < v:
                self.seen[id(sem)] = v
                self.todo.append((0, sem, v))

    def put(self, fn, *after):
        self.wait(after)
        self.n += 1
        self.todo.append((1, fn, (self.sem, 1)))
        return self.sem, self.n

    def then(self, fn, *after):
        return self.put(fn, (self.sem, self.n) if self.n else None, *after)

    def run(self, eng):
        for kind, a, b in self.todo:
            if kind == 0:
                eng.wait_ge(a, b)
            elif kind == 2:
                a()
            else:
                a().then_inc(*b)


class Ring:

    def __init__(self, sems):
        self.sems, self.v = sems, [0] * len(sems)

    def start(self, line, slot, fn, *after):
        line.wait(after)
        self.v[slot] += 16
        line.todo.append((1, fn, (self.sems[slot], 16)))
        return self.sems[slot], self.v[slot]


class Bank:

    def __init__(self, t):
        self.t, self.tok, self.busy = t, None, False

    def take(self):
        while self.busy:
            yield
        self.busy = True

    def give(self, tok):
        self.tok, self.busy = tok, False


class Tasks:

    def __init__(self):
        self.live = []

    def start(self, gen):
        self.live.append(gen)

    def turn(self):
        for g in list(self.live):
            if next(g, self) is self:
                self.live.remove(g)


E30 = 10686474581524.463


def build(nc, xtok, fT, cst, svec, cond, rms, rout, gatew, W0, W1, Y1):
    with ExitStack() as ctx:
        ctx.enter_context(nc.allow_low_precision(reason="sums of at most 16 ones are exact in float16"))

        def sb(name, shape, dt=F32):
            return ctx.enter_context(nc.sbuf_tensor(name, shape, dt))

        def sem(name):
            return ctx.enter_context(nc.semaphore(name))

        def ring(name, n):
            return Ring([sem(f"{name}{i}") for i in range(n)])

        X = [nc.dram_tensor(f"xrows{l}", [ROWS, D + LAYERS[l]["E"]], F32, kind="Internal").ap() for l in range(2)]
        Y0 = nc.dram_tensor("y0rows", [ROWS, D], F32, kind="Internal").ap()
        Y = [Y0, Y1]

        psG = [[ctx.enter_context(nc.psum_tensor(f"psG{a}{c}", [P, 512], F32)) for c in range(2)] for a in range(2)]
        psX = ctx.enter_context(nc.psum_tensor("psX", [P, 512], F32))
        psH = ctx.enter_context(nc.psum_tensor("psH", [P, 512], F32))
        psO = [ctx.enter_context(nc.psum_tensor(f"psO{a}", [P, 512], F32)) for a in range(2)]

        C = sb("C", [P, 528])
        ident, iota, U32f, dconst, tid = C[:, 0:128], C[:, 128:256], C[:, 256:384], C[:, 384:512], C[:, 512:528]
        iota16 = sb("iota16", [P, 128], F16)
        U16 = sb("U16", [P, 128], F16)
        ones16 = sb("ones16", [P, 128], F16)
        ones = sb("ones", [P, 8])
        half = sb("half", [P, 1])
        sv = sb("sv", [P, 16])
        rmsb = sb("rmsb", [P, D])
        rw = [sb("rw0", [P, 4, 8]), sb("rw1", [P, 4, 32])]
        dec = sb("dec", [P, 2, 4, 4])
        cs = sb("cs", [P, 8, 8])

        Whi = sb("Whi", [P, 8 * 3072], F16)
        Wlo = sb("Wlo", [P, 8 * 3072], F16)
        ST = [sb(f"ST{i}", [P, 1088]) for i in range(2)]

        WK = [{n: sb(f"wk{n}{i}", [P, 512]) for n in ("K", "EK", "EU", "EKV", "NF", "DF")} for i in range(2)]
        RT = [sb(f"RT{i}", [P, 4, 512]) for i in range(2)]
        XT = [sb(f"XT{i}", [P, 512]) for i in range(4)]
        BS = sb("BS", [P, 512])
        XR = [sb(f"XR{i}", [P, 512]) for i in range(2)]
        HT32 = sb("HT32", [P, 512])
        cnd = HT32[:, :].rearrange("p (b k) -> p b k", b=4)
        sm = sb("sm", [P, NT, 4])
        XSp = [sb(f"XSp{i}", [P, 2, 512], F16) for i in range(4)]
        XG = [sb(f"XG{i}", [P, D + 32]) for i in range(3)]
        zero = XG[0]
        WSL = sb("WSL", [P, 8])
        jnk = sb("jnk", [P, 8])
        H32 = [sb(f"H32{i}", [P, 384]) for i in range(2)]
        HS = [sb(f"HS{i}", [P, 2, 384], F16) for i in range(2)]
        OB = [sb(f"OB{i}", [P, 512]) for i in range(4)]

        lg = sb("lg", [P, 4, 32])
        mx = sb("mx", [P, 4, 8])
        ix = sb("ix", [P, 4, 8], U32)
        ixf = sb("ixf", [P, 4, 8])
        ex = sb("ex", [P, 4, 32])
        et = sb("et", [P, 4, 8])
        s1 = sb("s1", [P, 4, 1])
        s2 = sb("s2", [P, 4, 1])
        OH = sb("OH", [P, 4 * 6 * 32])
        OT = sb("OT", [P, 4 * 6 * 32])
        mask = sb("mask", [P, 4, 32], F16)
        mred = sb("mred", [P, 32], F16)
        macc = [sb(f"macc{i}", [P, 32], F16) for i in range(5)]
        Wd = [sb(f"Wd{i}", [P, 4, 32]) for i in range(2)]
        posb = sb("posb", [P, 16 * 8])
        gq = sb("gq", [P, 96])
        gi = sb("gi", [P, 96], I32)
        gj = sb("gj", [P, 96])
        qa = sb("qa", [P, 96])
        ja = sb("ja", [P, 96])
        cn = sb("cn", [P, 4, 8])
        cni = sb("cni", [P, 8], I32)
        ebf = sb("ebf", [P, 39])
        ebi = gi[:, 48:87]
        ohB = sb("ohB", [P, 39, 8], F16)
        AB = [RT[1][:, i, :].bitcast(F16).rearrange("p (a r n) -> p a r n", a=2, r=4) for i in range(2)]
        AB1 = [Whi[:, 21760 + 1024 * i:22784 + 1024 * i].rearrange("p (a r n) -> p a r n", a=2, r=4) for i in range(2)]
        idf = U32f
        idt = OT[:, 0:128]
        idx = [sb("idx0", [P, 39], U32), posb[:, :].bitcast(U32)]

        pe, act, dve, pool, sp = (Line(sem(n)) for n in ("s_pe", "s_act", "s_dve", "s_pool", "s_sp"))
        s_c, s_z = ring("s_c", 1), ring("s_z", 1)
        r_k, r_x, r_st, r_g, r_o = ring("r_k", 2), ring("r_x", 4), ring("r_st", 2), ring("r_g", 3), ring("r_o", 4)
        r_y = ring("r_y", 4)
        r_xr = [ring("r_xr0", 2), ring("r_xr1", 2)]
        r_wd = [ring("r_wd0", 2), ring("r_wd1", 2)]
        V, A, G = nc.vector, nc.scalar, nc.gpsimd
        S = nc.sync

        for dst, src in ((C[:, :], cst), (sv[:, :], svec), (cnd[:, :, :], cond), (rmsb[:, :], rms),
                         (rw[0][:, :, :], rout), (rw[1][:, :, :], gatew)):
            t_c = s_c.start(sp, 0, lambda d=dst, s=src: S.dma_start(d, s))
        t_z = dve.put(lambda: V.memset(zero[:, :], 0.0))
        dve.put(lambda: V.memset(ones16[:, :], 1.0))
        dve.put(lambda: V.memset(ones[:, :], 1.0))
        t_half = dve.put(lambda: V.memset(half[:, :], -0.5))
        for h in H32:
            dve.put(lambda h=h: V.memset(h[:, :], 0.0))
        dve.put(lambda: V.tensor_copy(iota16[:, :], iota), t_c)
        t_c16 = dve.put(lambda: V.tensor_copy(U16[:, :], U32f))
        t = dve.then(lambda: V.tensor_reduce(cs[:, 0, 0:4], cnd[:, :, :], AX_X, ALU.add), t_c)
        t = act.put(lambda: A.activation(cs[:, 1, 0:4], cs[:, 0, 0:4], ACT.Exp, scale=-1.0), t)
        t = dve.then(lambda: V.tensor_scalar(cs[:, 2, 0:4], cs[:, 1, 0:4], 1.0, None, ALU.add), t)
        t = dve.then(lambda: V.reciprocal(cs[:, 3, 0:4], cs[:, 2, 0:4]), t)
        dve.then(lambda: V.tensor_scalar(cs[:, 4, 0:4], cs[:, 3, 0:4], 0.5, 0.5, ALU.mult, ALU.add), t)
        t_cs = dve.then(lambda: V.tensor_scalar(cs[:, 5, 0:4], cs[:, 3, 0:4], 0.1, 0.4, ALU.mult, ALU.add))
        t = act.put(lambda: A.activation(cs[:, 6, :], sv[:, 0:8], ACT.Exp), t_c)
        t_w = act.put(lambda: A.activation(cs[:, 7, :], cs[:, 6, :], ACT.Exp, scale=-1.0), t)
        for l in range(2):
            for c in range(4):
                t_dec = dve.then(lambda l=l, c=c: V.tensor_scalar(dec[:, l, c, :], cs[:, 4, 0:4],
                                                                 cs[:, 7, 4 * l + c:4 * l + c + 1], None, ALU.mult),
                                t_w, t_cs)

        t_dummy = []

        def dummies():
            for k in range(4):
                rows = slice(T + P * k, T + P * k + P)
                for dst, w in ((X[0], D + 8), (X[1], D + 32), (Y[0], D), (Y[1], D)):
                    t = s_z.start(sp, 0, lambda d=dst, r=rows, w=w: S.dma_start(d[r, :], zero[:, 0:w]), t_z)
            t_dummy.append(t)

        wk = dict(n=0, half=0, done=0)
        wf = {}
        rt_ready, rt_free = {}, {(0, 0): [], (0, 1): []}

        def wkv(l, b, c, bank):
            n = wk["n"]
            wk["n"] += 1
            s = n % 2
            B = WK[s]
            k = B["K"]
            t_k = r_k.start(sp, s, lambda: S.dma_start(k[:, :], fT[c * P:c * P + P, b * 512:b * 512 + 512]),
                            wf.get(("k", n - 2)))
            u = sv[:, 8 + 4 * l + c:9 + 4 * l + c]
            dc = dec[:, l, c, b:b + 1].to_broadcast([P, 512])
            yield
            a0 = dve.put(lambda: V.tensor_scalar(B["EK"][:, :], k[:, :], 30.0, None, ALU.min), t_k, wf.get(("e", n - 2)))
            e1 = act.put(lambda: A.activation(B["EU"][:, :], k[:, :], ACT.Exp, bias=u), t_k, t_c, wf.get(("e", n - 2)))
            e0 = act.put(lambda: A.activation(B["EK"][:, :], B["EK"][:, :], ACT.Exp), a0)
            yield
            p0 = pool.put(lambda: G.tensor_tensor(B["EKV"][:, :], B["EK"][:, :], k[:, :], ALU.mult), e0, wf.get(("e", n - 2)))
            p1 = dve.put(lambda: V.scalar_tensor_tensor(out=B["EU"][:, :], in0=B["EU"][:, :], scalar=E30,
                                                        in1=B["EK"][:, :], op0=ALU.min, op1=ALU.subtract), e0, e1)
            p2 = pool.put(lambda: G.tensor_tensor(k[:, :], B["EU"][:, :], k[:, :], ALU.mult), p1, p0)
            yield
            while n >= 2 and ("d", n - 2) not in wf:
                yield
            dve.put(lambda: V.tensor_tensor_scan(B["DF"][:, :], dc, B["EK"][:, :], 0.0, ALU.mult, ALU.add), e0, t_dec, wf.get(("d", n - 2)))
            d1 = dve.then(lambda: V.tensor_tensor_scan(B["EK"][:, ::-1], dc, B["EK"][:, ::-1], 0.0, ALU.mult, ALU.add), p0)
            t1 = pool.put(lambda: G.tensor_tensor(B["DF"][:, :], B["DF"][:, :], B["EK"][:, :], ALU.add), d1)
            t2 = pool.put(lambda: G.tensor_tensor(B["DF"][:, :], B["DF"][:, :], B["EU"][:, :], ALU.add), t1)
            yield
            while n >= 2 and ("m", n - 2) not in wf:
                yield
            dve.put(lambda: V.tensor_tensor_scan(B["NF"][:, :], dc, B["EKV"][:, :], 0.0, ALU.mult, ALU.add), p0, wf.get(("m", n - 2)))
            d3 = dve.then(lambda: V.tensor_tensor_scan(B["EKV"][:, ::-1], dc, B["EKV"][:, ::-1], 0.0, ALU.mult, ALU.add))
            q0 = pool.put(lambda: G.tensor_tensor(B["NF"][:, :], B["NF"][:, :], B["EKV"][:, :], ALU.add), d3)
            q1 = pool.put(lambda: G.tensor_tensor(B["NF"][:, :], B["NF"][:, :], k[:, :], ALU.add), q0, p2)
            wf["k", n] = wf["e", n] = q1
            wk["half"] += 1
            yield
            t3 = dve.put(lambda: V.tensor_scalar(B["DF"][:, :], B["DF"][:, :], 1e-8, None, ALU.max), t2)
            t4 = dve.put(lambda: V.reciprocal(B["DF"][:, :], B["DF"][:, :]), t3)
            yield
            t5 = dve.put(lambda: V.scalar_tensor_tensor(out=B["NF"][:, :], in0=B["NF"][:, :], scalar=cs[:, 5, b:b + 1],
                                                        in1=B["DF"][:, :], op0=ALU.mult, op1=ALU.mult), t4, q1, t_cs)
            wf["d", n] = t5
            yield
            h = b % 2
            while (l, b) not in rt_free:
                yield
            yield from bank.take()

            def tr():
                for q in range(4):
                    m = nc.tensor.transpose(bank.t[:, q * P:q * P + P], B["NF"][:, q * P:q * P + P], ident)
                return m
            m = pe.put(tr, t5, t_c, bank.tok)
            wf["m", n] = m
            yield
            e = act.put(lambda: A.copy(RT[h][:, :, c * P:c * P + P], bank.t[:, :].rearrange("p (q c) -> p q c", q=4)),
                        m, *rt_free[l, b])
            bank.give(e)
            wk["done"] += 1
            if c == 3:
                rt_ready[l, b] = e

        xs = dict(n=0, free=[None] * len(XSp))
        xt = dict(n=0, free=[None] * len(XT))
        fr = dict(xr=[(), ()], ht=None, hold=False, turned=0, lg={}, base=None)
        tile_xs, tile_x, lgt, xrow = {}, {}, {}, {}

        def load_x(l, i, *after):
            s = xt["n"] % len(XT)
            xt["n"] += 1
            src = (xtok if l == 0 else Y0)[i * P:i * P + P, :]
            tile_x[l, i] = (s, r_x.start(sp, s, lambda: S.dma_start(XT[s][:, :], src), xt["free"][s], *after))

        def front(l, i, bx, bl):
            s, t_x = tile_x[l, i]
            o = i % 2
            b, q = divmod(i, 4)
            R = XR[o]
            rt = RT[b % 2][:, q, :]
            E = LAYERS[l]["E"]
            a = act.put(lambda: A.activation(R[:, :], XT[s][:, :], ACT.Tanh, scale=0.5), t_x, *fr["xr"][o])
            yield
            a = dve.put(lambda: V.scalar_tensor_tensor(out=R[:, :], in0=R[:, :], scalar=1.0, in1=rt,
                                                       op0=ALU.add, op1=ALU.mult), a, rt_ready[l, b])
            fr["base"] = a
            fr["nbase", l] = i + 1
            if q == 3:
                nxt = (l, b + 2) if b < 2 else (1, b - 2)
                if l == 0 or b < 2:
                    rt_free[nxt] = [a]
            if l == 0:
                yield
                c = act.then(lambda: A.activation(BS[:, :], R[:, :], ACT.Square, accum_out=sm[:, i, 0:1]), a)
                yield
                c = dve.put(lambda: V.tensor_scalar(sm[:, i, 1:2], sm[:, i, 0:1], 1.0 / D, 1e-6, ALU.mult, ALU.add), c)
                c = pool.put(lambda: G.tensor_tensor(sm[:, i, 2:3], sm[:, i, 1:2], half[:, :], ALU.pow), c, t_half)
                yield
                a = dve.put(lambda: V.scalar_tensor_tensor(out=R[:, :], in0=R[:, :], scalar=sm[:, i, 2:3],
                                                           in1=rmsb[:, :], op0=ALU.mult, op1=ALU.mult), c, t_c)
            w = r_xr[l].start(sp, o, lambda: S.dma_start(X[l][i * P:i * P + P, 0:D], R[:, :]), a)
            xrow[l, i] = w
            yield
            yield from bx.take()
            while fr["hold"]:
                yield
            fr["hold"] = True

            def tr():
                for q in range(4):
                    m = nc.tensor.transpose(bx.t[:, q * P:q * P + P], R[:, q * P:q * P + P], ident)
                return m
            m = pe.put(tr, a, bx.tok, t_c)
            fr["xr"][o] = (w, m)
            fr["turned"] += 1
            yield
            z = xs["n"] % len(XSp)
            xs["n"] += 1
            c = act.put(lambda: A.copy(HT32[:, :], bx.t[:, :]), m, fr["ht"])
            h = act.put(lambda: A.activation(XSp[z][:, 0, :], bx.t[:, :], ACT.Copy, scale=XS), m, xs["free"][z])
            yield
            lo = dve.put(lambda: V.scalar_tensor_tensor(out=XSp[z][:, 1, :], in0=bx.t[:, :], scalar=XS,
                                                        in1=XSp[z][:, 0, :], op0=ALU.mult, op1=ALU.subtract), h)
            tile_xs[l, i] = (z, lo)
            bx.give(lo)
            yield from bl.take()

            def lgm():
                for q in range(4):
                    m = nc.tensor.matmul(bl.t[:, 0:E], HT32[:, q * P:q * P + P], rw[l][:, q, :],
                                         start=(q == 0), stop=(q == 3))
                return m
            m = pe.put(lgm, c, bl.tok, t_c)
            fr["ht"] = m
            fr["hold"] = False
            yield
            while q == 0 and b and (l, b - 1) not in fr["lg"]:
                yield
            t = dve.put(lambda: V.tensor_copy(lg[:, q, 0:E], bl.t[:, 0:E]), m, fr["lg"].get((l, b - 1)))
            bl.give(t)
            lgt[l, i] = t

        rb = dict(mask=None, mac=None)
        wd_tok = {0: [None, None], 1: [None, None]}

        def bc(ap, shape):
            return ap.to_broadcast(shape)

        def route(l, b, bl):
            L = LAYERS[l]
            E, K = L["E"], L["K"]
            for q in range(4):
                t = lgt[l, 4 * b + q]
                a = dve.then(lambda q=q: V.max(mx[:, q, :], lg[:, q, 0:E]), t)
                dve.then(lambda q=q: V.max_index(ix[:, q, :], mx[:, q, :], lg[:, q, 0:E]), a)
            yield
            psl = bl.t
            m0 = mx[:, :, 0:1]
            o = (OH[:, b * 64:b * 64 + 64] if l == 0 else OH[:, 0:4 * K * E]).rearrange("p (q k e) -> p q k e", q=4, k=K)
            ot = OT[:, 0:4 * K * E].rearrange("p (q k e) -> p q k e", q=4, k=K)
            a = dve.then(lambda: V.tensor_tensor(ex[:, :, 0:E], lg[:, :, 0:E], bc(m0, [P, 4, E]), ALU.subtract))
            c = dve.then(lambda: V.tensor_tensor(et[:, :, 0:K], mx[:, :, 0:K], bc(m0, [P, 4, K]), ALU.subtract))
            fr["lg"][l, b] = a
            a = act.put(lambda: A.activation(ex[:, :, 0:E], ex[:, :, 0:E], ACT.Exp), a)
            c = act.put(lambda: A.activation(et[:, :, 0:K], et[:, :, 0:K], ACT.Exp), c)
            x = dve.then(lambda: V.tensor_copy(ixf[:, :, 0:K], ix[:, :, 0:K]))
            x = dve.then(lambda: V.tensor_tensor(
                o, bc(iota[:, 0:E].unsqueeze(1).unsqueeze(1), [P, 4, K, E]),
                bc(ixf[:, :, 0:K].unsqueeze(3), [P, 4, K, E]), ALU.is_equal), x)
            yield
            mk = dve.then(lambda: V.tensor_reduce(mask[:, :, 0:E], o.rearrange("p q k e -> p q e k"), AX_X, ALU.add),
                         x, rb["mask"])
            a = dve.then(lambda: V.tensor_reduce(s1[:, :, :], ex[:, :, 0:E], AX_X, ALU.add), a)
            a = dve.then(lambda: V.reciprocal(s1[:, :, :], s1[:, :, :]), a)
            yield
            if l == 1:
                a = dve.then(lambda: V.tensor_scalar(s1[:, :, :], s1[:, :, :], UN, None, ALU.mult), a)
            a = dve.then(lambda: V.tensor_tensor(et[:, :, 0:K], et[:, :, 0:K], bc(s1[:, :, :], [P, 4, K]), ALU.mult), a, c)
            if l == 0:
                a = dve.then(lambda: V.tensor_reduce(s2[:, :, :], et[:, :, 0:K], AX_X, ALU.add), a)
                a = dve.then(lambda: V.reciprocal(s2[:, :, :], s2[:, :, :]), a)
                a = dve.then(lambda: V.tensor_scalar(s2[:, :, :], s2[:, :, :], UN, None, ALU.mult), a)
                a = dve.then(lambda: V.tensor_tensor(et[:, :, 0:K], et[:, :, 0:K], bc(s2[:, :, :], [P, 4, K]), ALU.mult), a)
            a = dve.then(lambda: V.tensor_tensor(ot, o, bc(et[:, :, 0:K].unsqueeze(3), [P, 4, K, E]), ALU.mult), a)
            a = dve.then(lambda: V.tensor_reduce(Wd[b % 2][:, :, 0:E], ot.rearrange("p q k e -> p q e k"), AX_X, ALU.add),
                        a, wd_tok[l][b % 2], wd_tok[0][b % 2])
            wd_tok[l][b % 2] = r_wd[l].start(sp, b % 2, lambda: S.dma_start(
                X[l][b * 512:b * 512 + 512, D:D + E].rearrange("(q p) e -> p q e", p=P), Wd[b % 2][:, :, 0:E]), a)
            yield
            n = dve.then(lambda: V.tensor_reduce(mred[:, 0:E], mask[:, :, 0:E].rearrange("p q e -> p e q"), AX_X, ALU.add), mk)
            if b == 0:
                n = dve.then(lambda: V.tensor_copy(macc[1][:, 0:E], mred[:, 0:E]), n, rb["mac"])
            else:
                n = dve.then(lambda: V.tensor_tensor(macc[b + 1][:, 0:E], macc[b][:, 0:E], mred[:, 0:E], ALU.add), n)

            def excl():
                for q in range(4):
                    outp = psl[:, q * E:q * E + E]
                    m = nc.tensor.matmul(outp, U16[:, :], mask[:, q, 0:E], start=True, stop=(q == 0 and b == 0))
                    for r in range(q):
                        m = nc.tensor.matmul(outp, ones16[:, :], mask[:, r, 0:E], start=False,
                                             stop=(r == q - 1 and b == 0))
                    if b:
                        m = nc.tensor.matmul(outp, ones16[:, :], macc[b][:, 0:E], start=False, stop=True)
                return m
            yield from bl.take()
            m = pe.put(excl, mk, n, t_c16, bl.tok)
            rb["mask"] = m
            rb["mac"] = m
            if l == 0:
                pb = posb[:, b * 32:b * 32 + 32]
                yield
                t = dve.then(lambda: V.tensor_copy(pb, psl[:, 0:32]), m)
                bl.give(t)
                rb["n", l] = b + 1
                return
            yield
            t = dve.then(lambda: V.tensor_tensor(
                ot, o, bc(psl[:, 0:4 * E].rearrange("p (q e) -> p q e", q=4).unsqueeze(2), [P, 4, K, E]), ALU.mult), m, a)
            bl.give(t)
            ks = slice(b * 4 * K, (b + 1) * 4 * K)
            t = dve.then(lambda: V.tensor_reduce(gq[:, ks].rearrange("p (q k) -> p q k", q=4), ot, AX_X, ALU.add), t)
            t = split_slot(ks, t)
            yield
            t = dve.then(lambda: V.scalar_tensor_tensor(out=ja[:, ks].rearrange("p (q k) -> p q k", q=4),
                                                       in0=ixf[:, :, 0:K], scalar=4.0,
                                                       in1=gj[:, ks].rearrange("p (q k) -> p q k", q=4),
                                                       op0=ALU.mult, op1=ALU.add), t)
            t = dve.then(lambda: V.tensor_scalar(gj[:, ks], gq[:, ks], float(CAP), -1000.0, ALU.is_ge, ALU.mult), t)
            rb["slots"] = dve.then(lambda: V.tensor_tensor(qa[:, ks], qa[:, ks], gj[:, ks], ALU.add), t)
            yield
            yield from tables(1, bl, b)

        def split_slot(ks, t):
            t = dve.then(lambda: V.tensor_copy(gi[:, ks], gq[:, ks]), t)
            t = dve.then(lambda: V.tensor_single_scalar(gi[:, ks], gi[:, ks], 7, ALU.arith_shift_right), t)
            t = dve.then(lambda: V.tensor_copy(gj[:, ks], gi[:, ks]), t)
            return dve.then(lambda: V.scalar_tensor_tensor(out=qa[:, ks], in0=gj[:, ks], scalar=-128.0, in1=gq[:, ks],
                                                          op0=ALU.mult, op1=ALU.add), t)

        def starts0(bl):
            yield from bl.take()
            psl = bl.t
            m = pe.put(lambda: nc.tensor.matmul(psl[:, 0:8], ones16[:, :], macc[4][:, 0:8], start=True, stop=True),
                       bl.tok, rb["mac"], (dve.sem, dve.n))
            rb["mac"] = m
            t = dve.then(lambda: V.tensor_scalar(cni[:, :], psl[:, 0:8], 127.0, None, ALU.add), m)
            bl.give(t)
            yield
            t = dve.then(lambda: V.tensor_single_scalar(cni[:, :], cni[:, :], 7, ALU.arith_shift_right), t)
            t = dve.then(lambda: V.tensor_copy(cn[:, 0, :], cni[:, :]), t)
            t = dve.then(lambda: V.tensor_tensor_scan(cn[:, 1, :], ones[:, :], cn[:, 0, :], 0.0, ALU.mult, ALU.add), t)
            t = dve.then(lambda: V.tensor_tensor(cn[:, 2, :], cn[:, 1, :], cn[:, 0, :], ALU.subtract), t)
            t = dve.then(lambda: V.tensor_scalar(cn[:, 2, :], cn[:, 2, :], 128.0, None, ALU.mult), t)
            pv = posb[:, :].rearrange("p (i e) -> p i e", i=16)
            ov = OH[:, 0:256].rearrange("p (i k e) -> p i k e", i=16, k=2)
            t = dve.then(lambda: V.tensor_tensor(pv, pv, bc(cn[:, 2:3, :], [P, 16, 8]), ALU.add), t)
            t = dve.then(lambda: V.tensor_tensor(ov, ov, bc(pv.unsqueeze(2), [P, 16, 2, 8]), ALU.mult), t)
            ks = slice(0, 32)
            t = dve.then(lambda: V.tensor_reduce(gq[:, ks].rearrange("p (i k) -> p i k", i=16), ov, AX_X, ALU.add), t)
            t = split_slot(ks, t)
            rb["slots"] = dve.then(lambda: V.tensor_copy(ja[:, ks], gj[:, ks]), t)
            yield
            u = dve.then(lambda: V.tensor_tensor(ohB[:, :, :], bc(cn[:, 1:2, :], [P, 39, 8]),
                                                bc(iota[:, 0:39].unsqueeze(2), [P, 39, 8]), ALU.is_le))
            u = dve.then(lambda: V.tensor_reduce(ebf[:, :].unsqueeze(2), ohB[:, :, :], AX_X, ALU.add), u)
            u = dve.then(lambda: V.tensor_scalar(ebf[:, :], ebf[:, :], 7.0, None, ALU.min), u)
            dve.then(lambda: V.tensor_copy(ebi, ebf[:, :]), u)
            u = dve.then(lambda: V.tensor_tensor(ohB[:, :, :], bc(iota[:, 0:8].unsqueeze(1), [P, 39, 8]),
                                                bc(ebf[:, :].unsqueeze(2), [P, 39, 8]), ALU.is_equal), u)
            rb["experts"] = u
            yield from tables(0, bl)

        def tables(l, bl, b=None):
            L = LAYERS[l]
            K, NB = L["K"], L["NB"]
            A16, B16 = [v[:, 0] for v in rb["onehots"]], [v[:, 1] for v in rb["onehots"]]
            t = rb["slots"]
            free = [None, None]
            yield from bl.take()
            psl = bl.t
            g0, ng = (0, 8) if l == 0 else (b * K, K)
            for g in range(ng):
                s = g % 2
                for r in range(4):
                    n = 4 * (g0 + g) + r
                    i = n // K
                    dve.put(lambda s=s, r=r, n=n: V.tensor_scalar(A16[s][:, r, :], iota16[:, :], qa[:, n:n + 1], None,
                                                                  ALU.is_equal), t, free[s], *rb["ab"])
                    d = dve.put(lambda s=s, r=r, n=n, i=i: V.tensor_scalar(
                        B16[s][:, r, 0:NB], iota16[:, 0:NB], ja[:, n:n + 1], tid[:, i:i + 1], ALU.is_equal, ALU.mult))
                yield

                def mm(g=g, s=s):
                    for r in range(4):
                        m = nc.tensor.matmul(psl[:, 0:NB], A16[s][:, r, :], B16[s][:, r, 0:NB],
                                             start=(g == 0 and r == 0), stop=(g == ng - 1 and r == 3))
                    return m
                free[s] = pe.put(mm, d, bl.tok)
            rb["ab"] = [free[0], free[1]]
            m = rb["tab"] = free[s]
            yield
            if l == 1:
                if b == 0:
                    t = dve.then(lambda: V.tensor_copy(idf[:, :], psl[:, 0:NB]), m)
                else:
                    t = dve.then(lambda: V.tensor_tensor(idf[:, :], psl[:, 0:NB], idf[:, :], ALU.add), m)
                bl.give(t)
                rb["n", l] = b + 1
                if b < 3:
                    return
                src = idf[:, :]
            else:
                src = psl[:, 0:NB]
            u = dve.then(lambda: V.scalar_tensor_tensor(out=idt[:, 0:NB], in0=src, scalar=0.0,
                                                        in1=dconst[:, 0:NB], op0=ALU.is_equal, op1=ALU.mult), m)
            t = dve.then(lambda: V.scalar_tensor_tensor(out=idx[l][:, 0:NB], in0=src, scalar=-1.0,
                                                        in1=idt[:, 0:NB], op0=ALU.add, op1=ALU.add), u)
            if l == 0:
                bl.give(t)
            rb["table", l] = t

        wt = dict(n=0, free=[None] * 2, ahead=None)
        wq = []

        def wadd(src, dst, pieces, after, low, said):
            wq.extend((src, dst, p, after, low, said) for p in pieces)

        def wstep():
            now, wt["ahead"] = wt["ahead"], None
            if wq:
                src, dst, (c0, cw), after, low, said = wq.pop(0)
                s = wt["n"] % 2
                wt["n"] += 1
                t = r_st.start(sp, s, lambda: S.dma_start(ST[s][:, 0:cw], src[:, c0:c0 + cw]), wt["free"][s])
                wt["ahead"] = (s, t, dst + c0, cw, after, low, said)
            if now:
                wsplit(*now)

        def wsplit(s, t, at, cw, after, low, said):
            st_, hi, lo = ST[s][:, 0:cw], Whi[:, at:at + cw], Wlo[:, at:at + cw]
            if low == "pool":
                a = act.put(lambda: A.activation(st_, st_, ACT.Copy, scale=WS), t)
                a = act.put(lambda: A.copy(hi, st_), a, after)
                a = pool.put(lambda: G.tensor_tensor(lo, st_, hi, ALU.subtract), a, after)
            else:
                a = act.put(lambda: A.activation(hi, st_, ACT.Copy, scale=WS), t, after)
                a = dve.put(lambda: V.scalar_tensor_tensor(out=lo, in0=st_, scalar=WS, in1=hi,
                                                           op0=ALU.mult, op1=ALU.subtract), a, after)
            wt["free"][s] = a
            said(a)

        def wflush():
            while wq or wt["ahead"]:
                wstep()

        blocks = []
        st = dict(g=0, h=[None, None], hs=[None, None], o=[None, None], ob=[None] * 4, sg=None,
                  gf=[None, None], chain=[], last=None, xg=[None] * 3, px=None, ph=None, lo=0, ended=0)

        def gather(n):
            if n >= len(blocks) or blocks[n]["kind"] != "routed" or "g" in blocks[n]:
                return
            B = blocks[n]
            l, j = B["l"], B["j"]
            s = st["g"] % 3
            st["g"] += 1
            w = D + LAYERS[l]["E"]
            B["xg"] = s
            B["g"] = r_g.start(pool, s, lambda: G.indirect_dma_start(
                out=XG[s][:, 0:w], out_offset=None, in_=X[l][:, :],
                in_offset=bass.IndirectOffsetOnAxis(ap=idx[l][:, j:j + 1], axis=0)), B["ready"], *t_dummy, *B["rows"],
                *(st["xg"][s] or ()))

        def turn(n):
            if n >= len(blocks) or blocks[n]["kind"] != "routed":
                return
            B = blocks[n]
            l, s, j = B["l"], B["xg"], B["j"]
            w = WSL[:, n % 8:n % 8 + 1]

            def tr():
                for q in range(4):
                    m = nc.tensor.transpose(psX[:, q * P:q * P + P], XG[s][:, q * P:q * P + P], ident)
                return m
            m = pe.put(tr, B["g"], st["px"])
            if l == 0:
                u = dve.put(lambda: V.tensor_tensor_reduce(jnk[:, :], XG[s][:, D:D + 8], ohB[:, j, :], 1.0, 0.0,
                                                           ALU.mult, ALU.add, w), B["g"], st.get("u"))
            else:
                e = j // 4
                u = dve.put(lambda: V.tensor_copy(w, XG[s][:, D + e:D + e + 1]), B["g"])
            st["u"] = u
            B["u"] = u
            st["xg"][s] = (m, u)
            z = xs["n"] % len(XSp)
            xs["n"] += 1
            h = act.put(lambda: A.activation(XSp[z][:, 0, :], psX[:, :], ACT.Copy, scale=XS), m, xs["free"][z])
            lo = dve.put(lambda: V.scalar_tensor_tensor(out=XSp[z][:, 1, :], in0=psX[:, :], scalar=XS,
                                                        in1=XSp[z][:, 0, :], op0=ALU.mult, op1=ALU.subtract), h)
            st["px"] = lo
            B["xs"] = (z, lo)

        def gu(n):
            B = blocks[n]
            l = B["l"]
            F = LAYERS[l]["F"]
            z, t = B["xs"]
            a = n % 2
            hx = XSp[z]

            def mm():
                if B.get("reg"):
                    j = B["j"]
                    r = nc.tensor.value_load(ebi[0:1, j:j + 1], min_val=0, max_val=7)
                    B["rv"] = r

                    def w(half, off, n):
                        return half[:, bass.ds(r * 3072 + off, n)]
                else:
                    def w(half, off, n):
                        return half[:, B["w"] + off:B["w"] + off + n]
                B["wf"] = w
                if l == 0:
                    outs = [(psG[a][0][:, 0:512], 0, 512)]
                else:
                    outs = [(psG[a][0][:, 0:F], 0, F), (psG[a][1][:, 0:F], F, F)]
                for q in range(4):
                    off = q * 2 * F
                    for x, half in ((0, Whi), (0, Wlo), (1, Whi)):
                        first, last = q == 0 and x == 0 and half is Whi, q == 3 and x == 1
                        for o, c, nn in outs:
                            m = nc.tensor.matmul(o, hx[:, x, q * P:q * P + P], w(half, off + c, nn),
                                                 start=first, stop=last)
                return m
            m = pe.put(mm, t, st["gf"][a], *B["wt"])
            B["gu"] = m
            if B.get("endx", True):
                xs["free"][z] = m
            post.append(lambda: gu_ew(n, m))

        def gu_ew(n, m):
            B = blocks[n]
            l, a = B["l"], n % 2
            F = LAYERS[l]["F"]
            g, u = (psG[a][0][:, 0:F], psG[a][0][:, F:2 * F]) if l == 0 else (psG[a][0][:, 0:F], psG[a][1][:, 0:F])
            H = H32[a][:, 0:F]
            s = act.put(lambda: A.activation(H, g, ACT.Tanh, scale=0.5 * UN), m, st["h"][a])
            s = dve.put(lambda: V.scalar_tensor_tensor(out=H, in0=H, scalar=1.0, in1=g, op0=ALU.add, op1=ALU.mult), s)
            h = dve.put(lambda: V.scalar_tensor_tensor(out=H, in0=H, scalar=0.5 * XS * UN * UN, in1=u,
                                                       op0=ALU.mult, op1=ALU.mult), s)
            st["gf"][a] = h
            B["h"] = h

        def hturn(n):
            B = blocks[n]
            a = n % 2
            NK = LAYERS[B["l"]]["NK"]

            def tr():
                for q in range(NK):
                    m = nc.tensor.transpose(psH[:, q * P:q * P + P], H32[a][:, q * P:q * P + P], ident)
                return m
            m = pe.put(tr, B["h"], st["ph"])
            st["h"][a] = m
            post.append(lambda: hturn_ew(n, m))

        def hturn_ew(n, m):
            B = blocks[n]
            a = n % 2
            w = LAYERS[B["l"]]["NK"] * P
            h = act.put(lambda: A.copy(HS[a][:, 0, 0:w], psH[:, 0:w]), m, st["hs"][a])
            lo = dve.put(lambda: V.tensor_tensor(HS[a][:, 1, 0:w], psH[:, 0:w], HS[a][:, 0, 0:w], ALU.subtract), h)
            st["ph"] = lo
            B["hs"] = lo

        def down(n):
            B = blocks[n]
            l, a = B["l"], n % 2
            L = LAYERS[l]
            NK = L["NK"]
            o = B.get("bank", B["o"] % 2)
            off0 = 8 * L["F"]

            def mm():
                for q in range(NK):
                    for x, half in ((0, Whi), (0, Wlo), (1, Whi)):
                        m = nc.tensor.matmul(psO[o][:, :], HS[a][:, x, q * P:q * P + P],
                                             B["wf"](half, off0 + q * 512, 512),
                                             start=(q == 0 and x == 0 and half is Whi and B["first"]),
                                             stop=(q == NK - 1 and x == 1 and B["last"]))
                return m
            m = pe.put(mm, B["hs"], st["o"][o] if B["first"] else None)
            st["hs"][a] = m
            B["done"] = m
            st["done"] = m
            if B["last"]:
                post.append(lambda: down_ew(n, m))

        def down_ew(n, m):
            B = blocks[n]
            l = B["l"]
            o = B.get("bank", B["o"] % 2)
            k = B["o"] % 4
            if B["kind"] == "shared":
                s, _ = tile_x[l, B["i"]]
                i = B["i"]
                t = dve.put(lambda: V.scalar_tensor_tensor(out=OB[k][:, :], in0=psO[o][:, :], scalar=UN,
                                                           in1=XT[s][:, :], op0=ALU.mult, op1=ALU.add), m, st["ob"][k])
                xt["free"][s] = t
                w = r_y.start(sp, k, lambda: S.dma_start(Y[l][i * P:i * P + P, :], OB[k][:, :]), t)
                st["chain"].append(w)
                st["ended"] = i + 1
            else:
                j = B["j"]
                t = act.put(lambda: A.activation(OB[k][:, :], psO[o][:, :], ACT.Copy,
                                                 scale=WSL[:, n % 8:n % 8 + 1]), m, B["u"], st["ob"][k])
                if l == 0 or j % 4 == 0:
                    st["cur"] = st["chain"]
                    st["chain"] = []
                w = r_o.start(pool, k, lambda: G.indirect_dma_start(
                    out=Y[l][:, :], out_offset=bass.IndirectOffsetOnAxis(ap=idx[l][:, j:j + 1], axis=0),
                    in_=OB[k][:, :], in_offset=None, compute_op=ALU.add), t, *t_dummy, *st["cur"])
                st["chain"].append(w)
            st["o"][o] = t
            st["ob"][k] = w

        post = []

        def drain():
            while post:
                post.pop(0)()

        def step(n):
            gather(n + 3)
            turn(n + 1)
            gu(n)
            tasks.turn()
            drain()
            rest(n)
            drain()

        def rest(n):
            if n - 1 >= st["lo"]:
                hturn(n - 1)
            if n - 2 >= st["lo"]:
                down(n - 2)

        def flush():
            n = len(blocks)
            drain()
            hturn(n - 1)
            down(n - 2)
            drain()
            down(n - 1)
            drain()
            st["lo"] = n

        no = [0]

        def add(**kw):
            kw.setdefault("first", True)
            kw.setdefault("last", True)
            kw["o"] = no[0]
            if kw["last"]:
                no[0] += 1
            blocks.append(kw)
            return len(blocks) - 1

        tasks = Tasks()
        bX, bF, bL, bO = Bank(psX), Bank(psG[0][1]), Bank(psG[1][1]), Bank(psO[1])
        rb["ab"] = []
        rb["onehots"] = AB

        def fronts(l, wkvs, bw, bx, bl, done, xready, shared, weights, after_fronts, after_shared):
            st["ended"] = 0
            xt["base"] = xt["n"]
            nf = ns = nr = nx = 0
            live = []
            routing = [None]
            rb["n", l] = 0
            fr["nbase", l] = 0
            tailed = False

            def counted(gen, what):
                yield from gen
                what[0] += 1
            fin = [0]
            t0 = fr["turned"]
            while ns < NT or not tailed or tasks.live:
                if wkvs and wk["n"] - wk["half"] < 2:
                    tasks.start(wkv(*wkvs.pop(0), bw))
                while nx < NT and nx < st["ended"] + 4 and nx <= nf + 2:
                    load_x(l, nx, *xready)
                    nx += 1
                if nf < nx and nf - (fr["turned"] - t0) < 2 and (l, nf // 4) in rt_ready:
                    tasks.start(counted(front(l, nf, bx, bl), fin))
                    nf += 1
                if nr < 4 and fin[0] >= 4 * nr + 4 and rb["n", l] == nr:
                    tasks.start(route(l, nr, bl))
                    nr += 1
                if not tailed and rb["n", l] == 4:
                    tasks.start(after_fronts())
                    tailed = True
                tasks.turn()
                drain()
                weights()
                if l == 0:
                    tasks.turn()
                    if ns == 0:
                        tasks.turn()
                if ns < NT and (l, ns) in tile_xs:
                    shared(ns)
                    ns += 1
                    if ns == NT:
                        flush()
                        after_shared()

        wsh, w0 = [], []
        wadd(W0[8], 7 * 3072, WCH[0], None, "dve", wsh.append)
        for e in range(7):
            wadd(W0[e], e * 3072, WCH[0], None, "pool", w0.append)
        cnt = [0, 0]

        def weights0():
            if not t_dummy:
                dummies()
            cnt[0] += 1
            if cnt[0] % 2 == 0 or cnt[1]:
                wstep()

        def shared0(i):
            n = add(kind="shared", l=0, i=i, xs=tile_xs[0, i], w=7 * 3072, wt=[wsh[-1]])
            gu(n)
            rest(n)


        def last0():
            wadd(W0[7], 7 * 3072, WCH[0], st["done"], "pool", w0.append)
            cnt[1] = 1

        def tail0():
            RTlast = [fr["base"]]
            rb["ab"] = RTlast
            yield from starts0(bL)

        fronts(0, [(0, b, c) for b in range(4) for c in range(4)], bX, bF, bL, None, [], shared0, weights0, tail0, last0)
        wflush()
        rt_free[1, 1] = [fr["base"], rb["tab"]]
        base = len(blocks)
        rows = [xrow[0, 14], xrow[0, 15]] + wd_tok[0]
        for j in range(39):
            add(kind="routed", l=0, j=j, reg=True, ready=rb["table", 0], rows=rows, wt=[w0[-1], rb["experts"]])
        for n in (base, base + 1, base + 2):
            gather(n)
        st["px"] = bX.tok
        turn(base)
        todo = [(1, b, c) for b in range(2) for c in range(4)]
        for n in range(base, base + 39):
            if todo and wk["n"] - wk["half"] < 2:
                tasks.start(wkv(*todo.pop(0), bF))
            step(n)
        while tasks.live or todo:
            if todo and wk["n"] - wk["half"] < 2:
                tasks.start(wkv(*todo.pop(0), bF))
            tasks.turn()
        flush()
        end0 = st["done"]
        done0 = list(st["chain"])

        st["chain"] = []
        order = [32, 33] + list(range(32))
        slot = {e: (m % 5) * 4352 for m, e in enumerate(order)}
        wtok, last_use = {}, {}

        parts = {}

        def split_in(e, t):
            wtok[e] = t
            parts[e] = parts.get(e, 0) + 1

        def load1(m, *pieces):
            e = order[m]
            after = end0 if m < 5 else last_use[order[m - 5]]
            wadd(W1[e], slot[e], [WCH[1][p] for p in pieces], after, "pool" if 2 <= m < 5 else "dve", lambda t: split_in(e, t))

        for m in range(5):
            load1(m, 0, 1, 2, 3)
        for _ in range(2):
            wstep()
        rb["onehots"] = AB1
        rb["ab"] = [end0]
        bX.tok = st["px"]
        bO.tok = st["o"][1]
        cnt = [0]

        def weights1():
            cnt[0] += 1
            if cnt[0] <= 9 or cnt[0] % 3 == 0:
                wstep()

        def shared1(i):
            while parts.get(33, 0) < 4:
                wstep()
            for hf in range(2):
                n = add(kind="shared", l=1, i=i, xs=tile_xs[1, i], w=slot[32 + hf], wt=[wtok[32 + hf]], bank=0,
                        first=(hf == 0), last=(hf == 1), endx=(hf == 1))
                gu(n)
                tasks.turn()
                drain()
                rest(n)
                tasks.turn()
                drain()
            if i >= 1:
                wstep()


        fronts(1, [(1, b, c) for b in (2, 3) for c in range(4)], bX, bX, bO, None, done0, shared1, weights1,
               lambda: iter(()), wflush)
        st["o"][1] = bO.tok
        st["px"] = bX.tok
        base = len(blocks)
        rows = [xrow[1, 14], xrow[1, 15]] + wd_tok[1]
        for j in range(128):
            add(kind="routed", l=1, j=j, ready=rb["table", 1], rows=rows, w=slot[j // 4])
        for n in (base, base + 1, base + 2):
            gather(n)
        turn(base)
        for g in range(128):
            n = base + g
            blocks[n]["wt"] = [wtok[g // 4]]
            step(n)
            if g == 2:
                last_use[32] = last_use[33] = blocks[base - 1]["done"]
            if g % 4 == 2 and g > 4:
                last_use[g // 4 - 1] = blocks[base + g - 3]["done"]
            if g == 3:
                load1(5, 0, 1, 2, 3)
                load1(6, 0, 1, 2, 3)
            if g % 4 == 3 and 7 <= 6 + g // 4 < 34:
                load1(6 + g // 4, 0, 1, 2, 3)
            if g >= 3:
                wstep()
            if g < 12:
                wstep()
        flush()
        last = [(r_o.sems[k], r_o.v[k]) for k in range(4)] + [(r_y.sems[k], r_y.v[k]) for k in range(4)]
        sp.wait(last)

        block = ctx.enter_context(nc.Block())

        @block.sync
        def _(eng):
            sp.run(eng)

        @block.gpsimd
        def _(eng):
            pool.run(eng)

        @block.scalar
        def _(eng):
            act.run(eng)

        @block.vector
        def _(eng):
            dve.run(eng)

        @block.tensor
        def _(eng):
            pe.run(eng)


def kernel(**inputs):
    import numpy as np
    import concourse.bacc as bacc
    from concourse.bass_utils import run_bass_kernel_spmd

    f = {k: np.asarray(v) for k, v in inputs.items()}
    x = np.ascontiguousarray(f["x"].reshape(2048, 512))
    fT = np.ascontiguousarray(f["fside_BxSxS_0"].reshape(2048, 512).T)
    cst = np.zeros((128, 528), np.float32)
    p = np.arange(128)
    cst[:, 0:128] = np.eye(128)
    cst[:, 128:256] = p[None, :]
    cst[:, 256:384] = p[:, None] < p[None, :]
    cst[:, 384:512] = 2049 + 128 * (p[None, :] % 4) + p[:, None]
    cst[:, 512:528] = 128 * np.arange(16)[None, :] + p[:, None] + 1

    def cols(v):
        return v.reshape(4, 128).T

    svec = np.ascontiguousarray(np.concatenate(
        [cols(f[n]) for n in ("L0_cond_w", "L1_cond_w", "L0_cond_u", "L1_cond_u")], axis=1))
    cond = np.ascontiguousarray(np.broadcast_to(f["cond_512"][None], (128, 4, 128)))
    rms = np.ascontiguousarray(np.broadcast_to(f["L0_ffn_rms_weight"][None], (128, 512)))
    rout = np.ascontiguousarray(f["L0_ffn_router_w"].reshape(4, 128, 8).transpose(1, 0, 2))
    gatew = np.ascontiguousarray(f["L1_ffn_gate_w"].T.reshape(4, 128, 32).transpose(1, 0, 2))

    def pack(gate, up, downw, nk):
        e, _, F = gate.shape
        gu = np.concatenate([gate, up], axis=2).reshape(e, 4, 128, 2 * F).transpose(0, 2, 1, 3).reshape(e, 128, 8 * F)
        dp = np.zeros((e, nk * 128, 512), np.float32)
        dp[:, :F] = downw
        dp = dp.reshape(e, nk, 128, 512).transpose(0, 2, 1, 3).reshape(e, 128, nk * 512)
        return np.ascontiguousarray(np.concatenate([gu, dp], axis=2))

    W0 = pack(np.concatenate([f["L0_ffn_w_gate"], f["L0_ffn_sw_gate"][None]]),
              np.concatenate([f["L0_ffn_w_up"], f["L0_ffn_sw_up"][None]]),
              np.concatenate([f["L0_ffn_w_down"], f["L0_ffn_sw_down"][None]]), 2)

    def halves(a):
        return a.reshape(512, 2, 352).transpose(1, 0, 2)

    W1 = pack(np.concatenate([f["L1_ffn_w1"], halves(f["L1_ffn_sw1"])]),
              np.concatenate([f["L1_ffn_w3"], halves(f["L1_ffn_sw3"])]),
              np.concatenate([f["L1_ffn_w2"], f["L1_ffn_sw2"].reshape(2, 352, 512)]), 3)

    nc = bacc.Bacc("TRN2", target_bir_lowering=False, num_devices=1)
    arrays, args = {}, []
    for name, a in (("x", x), ("fT", fT), ("cst", cst), ("svec", svec), ("cond", cond), ("rms", rms),
                    ("rout", rout), ("gatew", gatew), ("W0", W0), ("W1", W1)):
        arrays[name] = a
        args.append(nc.dram_tensor(name, list(a.shape), mybir.dt.from_np(a.dtype), kind="ExternalInput").ap())
    out = nc.dram_tensor("out", [ROWS, D], F32, kind="ExternalOutput").ap()
    build(nc, *args, out)
    r = run_bass_kernel_spmd(nc, [arrays], core_ids=[0])
    return r.results[0]["out"][:2048].reshape(4, 512, 512)
```
